# Optimizing a Trainium2 kernel written in Bass

```python
import numpy as np
import jax
import jax.numpy as jnp

def _softmax(x, axis=-1):
    return jax.nn.softmax(x, axis=axis)

def _gelu(x):
    return jax.nn.gelu(x, approximate=True)

def _silu(x):
    return jax.nn.silu(x)

def _sigmoid(x):
    return jax.nn.sigmoid(x)

def _layernorm(x, axis=-1, eps=1e-05):
    m = jnp.mean(x, axis=axis, keepdims=True)
    v = jnp.var(x, axis=axis, keepdims=True)
    return (x - m) / jnp.sqrt(v + eps)

def _scatter_add(tgt, idx, src, axis=0):
    return tgt.at[idx].add(src)

def _segment_sum(src, seg, n):
    return jax.ops.segment_sum(src, seg, n)
kernel_name = 'mk_gnn_resnorm_d2_gnn_r8_f9068b'

def setup_inputs(seed: int=0):
    np.random.seed(seed)
    _w = jnp.asarray

    def _rec_inputs():
        import jax
        import jax.numpy as jnp
        _gk = jax.random.key(seed)
        x = -0.0009044 + 1 * jax.random.normal(jax.random.fold_in(_gk, 1), (12500, 160), jnp.float32)
        _s = jax.random.randint(jax.random.fold_in(_gk, 2), (100000,), 0, 12500, jnp.int32)
        _d = jax.random.randint(jax.random.fold_in(_gk, 3), (100000,), 0, 12500, jnp.int32)
        _loop = jnp.arange(12500, dtype=jnp.int32)
        src = jnp.concatenate([_s, _d, _loop])
        dst = jnp.concatenate([_d, _s, _loop])
        _o = jnp.argsort(dst, stable=True)
        src = src[_o]
        dst = dst[_o]
        edge_attr_3 = 0.00262751 + 0.999568 * jax.random.normal(jax.random.fold_in(_gk, 12), (212500, 3), jnp.float32)
        edge_attr_4 = 0.0012443 + 1.0001 * jax.random.normal(jax.random.fold_in(_gk, 13), (212500, 4), jnp.float32)
        edge_attr_64 = jax.random.uniform(jax.random.fold_in(_gk, 14), (212500, 64), jnp.float32, 0.0, 1)
        node_vec1 = jax.random.uniform(jax.random.fold_in(_gk, 15), (12500, 1), jnp.float32, 0.0, 1)
        return (x, src, dst, edge_attr_3, edge_attr_4, edge_attr_64, node_vec1)
    x, src, dst, edge_attr_3, edge_attr_4, edge_attr_64, node_vec1 = _rec_inputs()

    def _L0_gnn_setup():
        import jax, jax.numpy as jnp
        import numpy as np
        N, E = (1250, 20000)
        C0, C1 = (64, 32)
        H, A = (8, 8)
        H0, H1 = (8, 4)
        M0, M1 = (128, 64)
        NG, RH = (64, 64)
        WN = C0 + C0 + C1 + C1 + C1
        DS, DV = (C0 + C1, C0 + 2 * C1)
        EPS = 1e-05
        SQ3 = np.float32(np.sqrt(3.0))
        SQ2 = np.float32(np.sqrt(2.0))

        def _split(x):
            return (x[:, :C0], x[:, C0:].reshape(x.shape[0], C1, 3))

        def _merge(s, v):
            return jnp.concatenate([s, v.reshape(v.shape[0], -1)], axis=1)

        def _eq_ln(x, w0, b0, w1):
            s, v = _split(x)
            s = s - s.mean(axis=1, keepdims=True)
            s = s * jax.lax.rsqrt(jnp.square(s).mean(axis=1, keepdims=True) + EPS) * w0 + b0
            v = v * jax.lax.rsqrt(jnp.square(v).mean(axis=(1, 2), keepdims=True) + EPS) * w1[None, :, None]
            return (s, v)

        def _eq_lin(s, v, ws, bs, wv):
            return (s @ ws + bs, jnp.einsum('nud,uk->nkd', v, wv))

        def _ln(x, g, b):
            xc = x - x.mean(-1, keepdims=True)
            return xc * jax.lax.rsqrt(jnp.square(xc).mean(-1, keepdims=True) + EPS) * g + b

        def _smooth_leaky(x, alpha=0.2):
            return 0.5 * (1 + alpha) * x + 0.5 * (1 - alpha) * x * (2.0 * jax.nn.sigmoid(x) - 1.0)

        def _forward(node_input, node_attr, edge_vec, edge_scalars, edge_src, edge_dst, ln1_w0, ln1_b0, ln1_w1, ln2_w0, ln2_b0, ln2_w1, msrc_ws, msrc_wv, mdst_ws, mdst_bs, mdst_wv, rw1, rb1, rg1, rbe1, rw2, rb2, rg2, rbe2, rw3, roff, lin_ws, lin_bs, lin_wv, alpha_dot, proj_ws, proj_bs, proj_wv, f1_ws, f1_bs, f1_wv, f2_ws, f2_bs, f2_wv):
            n = node_input.shape[0]
            s, v = _eq_ln(node_input, ln1_w0, ln1_b0, ln1_w1)
            src_s = s @ msrc_ws
            src_v = jnp.einsum('nud,uk->nkd', v, msrc_wv)
            dst_s = s @ mdst_ws + mdst_bs
            dst_v = jnp.einsum('nud,uk->nkd', v, mdst_wv)
            ms = src_s[edge_src] + dst_s[edge_dst]
            mv = src_v[edge_src] + dst_v[edge_dst]
            h = jax.nn.silu(_ln(edge_scalars @ rw1 + rb1, rg1, rbe1))
            h = jax.nn.silu(_ln(h @ rw2 + rb2, rg2, rbe2))
            w = h @ rw3 + roff
            rhat = edge_vec * jax.lax.rsqrt(jnp.sum(jnp.square(edge_vec), -1, keepdims=True) + 1e-12)
            Y1 = SQ3 * rhat
            w1, w2, w3, w4, w5 = jnp.split(w, [C0, 2 * C0, 2 * C0 + C1, 2 * C0 + 2 * C1], axis=1)
            o0a = w1 * ms
            o0b = w4 * (jnp.einsum('eud,ed->eu', mv, Y1) / SQ3)
            o1a = (w2 * ms)[:, :, None] * Y1[:, None, :]
            o1b = w3[:, :, None] * mv
            o1c = w5[:, :, None] * (jnp.cross(mv, Y1[:, None, :]) / SQ2)
            ds = jnp.concatenate([o0a, o0b], axis=1)
            dv = jnp.concatenate([o1a, o1b, o1c], axis=1)
            ls, lv = _eq_lin(ds, dv, lin_ws, lin_bs, lin_wv)
            e = ls.shape[0]
            alpha = ls[:, :H * A].reshape(e, H, A)
            vs = ls[:, H * A:].reshape(e, H, H0)
            vv = lv.reshape(e, H, H1, 3)
            a = jnp.einsum('ehk,hk->eh', _smooth_leaky(alpha), alpha_dot)
            amax = jax.lax.stop_gradient(jax.ops.segment_max(a, edge_dst, num_segments=n))
            a = jnp.exp(a - amax[edge_dst])
            a = a / (jax.ops.segment_sum(a, edge_dst, num_segments=n)[edge_dst] + 1e-12)
            ns = jax.ops.segment_sum(vs * a[..., None], edge_dst, num_segments=n).reshape(n, H * H0)
            nv = jax.ops.segment_sum(vv * a[..., None, None], edge_dst, num_segments=n).reshape(n, H * H1, 3)
            ps, pv = _eq_lin(ns, nv, proj_ws, proj_bs, proj_wv)
            x = node_input + _merge(ps, pv)
            s2, v2 = _eq_ln(x, ln2_w0, ln2_b0, ln2_w1)
            a0 = node_attr[:, :1]
            fs, fv = _eq_lin(s2, v2, f1_ws, f1_bs, f1_wv)
            fs = fs * a0
            fv = fv * a0[:, :, None]
            sc = jax.nn.silu(fs[:, :M0])
            fv = fv * jax.nn.sigmoid(fs[:, M0:])[:, :, None]
            os_, ov = _eq_lin(sc, fv, f2_ws, f2_bs, f2_wv)
            os_ = os_ * a0
            ov = ov * a0[:, :, None]
            return x + _merge(os_, ov)
        key = jax.random.key(seed)
        ks = iter(jax.random.split(key, 24))

        def nrm(shape, fan):
            return jax.random.normal(next(ks), shape, jnp.float32) / np.float32(np.sqrt(fan))
        inp = {}
        inp['node_input'] = jax.random.normal(next(ks), (N, C0 + 3 * C1), jnp.float32)
        inp['node_attr'] = jnp.ones((N, 1), jnp.float32)
        inp['edge_vec'] = jax.random.normal(next(ks), (E, 3), jnp.float32)
        inp['edge_scalars'] = jax.random.uniform(next(ks), (E, NG), dtype=jnp.float32)
        inp['edge_src'] = jax.random.randint(next(ks), (E,), 0, N)
        inp['edge_dst'] = jax.random.randint(next(ks), (E,), 0, N)
        inp['ln1_w0'] = jnp.ones((C0,), jnp.float32)
        inp['ln1_b0'] = jnp.zeros((C0,), jnp.float32)
        inp['ln1_w1'] = jnp.ones((C1,), jnp.float32)
        inp['ln2_w0'] = jnp.ones((C0,), jnp.float32)
        inp['ln2_b0'] = jnp.zeros((C0,), jnp.float32)
        inp['ln2_w1'] = jnp.ones((C1,), jnp.float32)
        inp['msrc_ws'] = nrm((C0, C0), C0)
        inp['msrc_wv'] = nrm((C1, C1), C1)
        inp['mdst_ws'] = nrm((C0, C0), C0)
        inp['mdst_bs'] = jnp.zeros((C0,), jnp.float32)
        inp['mdst_wv'] = nrm((C1, C1), C1)
        inp['rw1'] = nrm((NG, RH), NG)
        inp['rb1'] = jnp.zeros((RH,), jnp.float32)
        inp['rg1'] = jnp.ones((RH,), jnp.float32)
        inp['rbe1'] = jnp.zeros((RH,), jnp.float32)
        inp['rw2'] = nrm((RH, RH), RH)
        inp['rb2'] = jnp.zeros((RH,), jnp.float32)
        inp['rg2'] = jnp.ones((RH,), jnp.float32)
        inp['rbe2'] = jnp.zeros((RH,), jnp.float32)
        inp['rw3'] = nrm((RH, WN), RH)
        inp['roff'] = 0.1 * jax.random.normal(next(ks), (WN,), jnp.float32)
        inp['lin_ws'] = nrm((DS, H * A + H * H0), DS)
        inp['lin_bs'] = jnp.zeros((H * A + H * H0,), jnp.float32)
        inp['lin_wv'] = nrm((DV, H * H1), DV)
        inp['alpha_dot'] = nrm((H, A), A)
        inp['proj_ws'] = nrm((H * H0, C0), H * H0)
        inp['proj_bs'] = jnp.zeros((C0,), jnp.float32)
        inp['proj_wv'] = nrm((H * H1, C1), H * H1)
        inp['f1_ws'] = nrm((C0, M0 + M1), C0)
        inp['f1_bs'] = jnp.zeros((M0 + M1,), jnp.float32)
        inp['f1_wv'] = nrm((C1, M1), C1)
        inp['f2_ws'] = nrm((M0, C0), M0)
        inp['f2_bs'] = jnp.zeros((C0,), jnp.float32)
        inp['f2_wv'] = nrm((M1, C1), M1)
        return inp
    _L0_gnn_all = _L0_gnn_setup()
    _L0_gnn_in = {k: v for k, v in _L0_gnn_all.items() if k in ('ln1_w0', 'ln1_b0', 'ln1_w1', 'ln2_w0', 'ln2_b0', 'ln2_w1', 'msrc_ws', 'msrc_wv', 'mdst_ws', 'mdst_bs', 'mdst_wv', 'rw1', 'rb1', 'rg1', 'rbe1', 'rw2', 'rb2', 'rg2', 'rbe2', 'rw3', 'roff', 'lin_ws', 'lin_bs', 'lin_wv', 'alpha_dot', 'proj_ws', 'proj_bs', 'proj_wv', 'f1_ws', 'f1_bs', 'f1_wv', 'f2_ws', 'f2_bs', 'f2_wv')}
    del _L0_gnn_all

    def _L1_gnn_setup():
        import jax, jax.numpy as jnp
        import numpy as np
        N, E = (5000, 80000)
        S_IN, V_IN = (64, 32)
        S_MID, V_MID = (96, 128)
        S_OUT, V_OUT = (96, 32)
        R = 64
        FC_HID = 64
        W_NUMEL = 64 + 64 + 32 + 32 + 32
        NUM_NEIGHBORS = 16.0

        def _inv(d):
            return 1.0 / jnp.sqrt(jnp.float32(d))

        def _forward(node_features, node_attr, edge_attr, edge_scalars, lin1_ws, lin1_wv, fc_w1, fc_w2, sc_ws, sc_wv, lin2_ws, lin2_wv, edge_src, edge_dst):
            n = node_features.shape[0]
            s = node_features[:, :S_IN]
            v = node_features[:, S_IN:].reshape(n, V_IN, 3)
            a = node_attr
            sc_s = s @ sc_ws * a * _inv(S_IN)
            sc_v = jnp.einsum('nci,cd->ndi', v, sc_wv) * a[:, :, None] * _inv(V_IN)
            h_s = s @ lin1_ws * a * _inv(S_IN)
            h_v = jnp.einsum('nci,cd->ndi', v, lin1_wv) * a[:, :, None] * _inv(V_IN)
            hid = jax.nn.silu(edge_scalars @ fc_w1 * _inv(R))
            w = hid @ fc_w2 * _inv(FC_HID)
            w1, w2, w3, w4, w5 = jnp.split(w, [64, 128, 160, 192], axis=-1)
            es = h_s[edge_src]
            ev = h_v[edge_src]
            e0 = edge_attr[:, :1]
            e1 = edge_attr[:, 1:4]
            m_s1 = w1 * es * e0
            m_s2 = w4 * jnp.einsum('eci,ei->ec', ev, e1) * _inv(3)
            m_v1 = (w2 * es)[:, :, None] * e1[:, None, :]
            m_v2 = w3[:, :, None] * ev * e0[:, :, None]
            m_v3 = w5[:, :, None] * jnp.cross(ev, e1[:, None, :]) * _inv(2)
            mid_s = jnp.concatenate([m_s1, m_s2], axis=-1)
            mid_v = jnp.concatenate([m_v1, m_v2, m_v3], axis=1)
            inv_nn = 1.0 / jnp.sqrt(jnp.float32(NUM_NEIGHBORS))
            agg_s = jax.ops.segment_sum(mid_s, edge_dst, num_segments=n) * inv_nn
            agg_v = jax.ops.segment_sum(mid_v, edge_dst, num_segments=n) * inv_nn
            o_s = agg_s @ lin2_ws * a * _inv(S_MID)
            o_v = jnp.einsum('nci,cd->ndi', agg_v, lin2_wv) * a[:, :, None] * _inv(V_MID)
            pre_s = sc_s + o_s
            pre_v = sc_v + o_v
            scalars = jax.nn.silu(pre_s[:, :64])
            gates = jax.nn.sigmoid(pre_s[:, 64:96])
            gated = gates[:, :, None] * pre_v
            return jnp.concatenate([scalars, gated.reshape(n, 3 * V_OUT)], axis=-1)
        key = jax.random.key(seed)
        ks = jax.random.split(key, 13)
        return {'node_features': jax.random.normal(ks[0], (N, S_IN + 3 * V_IN), jnp.float32), 'node_attr': jnp.ones((N, 1), jnp.float32), 'edge_src': jax.random.randint(ks[1], (E,), 0, N), 'edge_dst': jax.random.randint(ks[2], (E,), 0, N), 'edge_attr': jax.random.normal(ks[3], (E, 4), jnp.float32), 'edge_scalars': jax.random.normal(ks[4], (E, R), jnp.float32), 'lin1_ws': jax.random.normal(ks[5], (S_IN, S_IN), jnp.float32), 'lin1_wv': jax.random.normal(ks[6], (V_IN, V_IN), jnp.float32), 'fc_w1': jax.random.normal(ks[7], (R, FC_HID), jnp.float32), 'fc_w2': jax.random.normal(ks[8], (FC_HID, W_NUMEL), jnp.float32), 'sc_ws': jax.random.normal(ks[9], (S_IN, S_OUT), jnp.float32), 'sc_wv': jax.random.normal(ks[10], (V_IN, V_OUT), jnp.float32), 'lin2_ws': jax.random.normal(ks[11], (S_MID, S_OUT), jnp.float32), 'lin2_wv': jax.random.normal(ks[12], (V_MID, V_OUT), jnp.float32)}
    _L1_gnn_all = _L1_gnn_setup()
    _L1_gnn_in = {k: v for k, v in _L1_gnn_all.items() if k in ('lin1_ws', 'lin1_wv', 'fc_w1', 'fc_w2', 'sc_ws', 'sc_wv', 'lin2_ws', 'lin2_wv')}
    del _L1_gnn_all
    return {'x': x, 'src': src, 'dst': dst, 'edge_attr_3': edge_attr_3, 'edge_attr_4': edge_attr_4, 'edge_attr_64': edge_attr_64, 'node_vec1': node_vec1, 'L0_gnn_ln1_w0': _L0_gnn_in['ln1_w0'], 'L0_gnn_ln1_b0': _L0_gnn_in['ln1_b0'], 'L0_gnn_ln1_w1': _L0_gnn_in['ln1_w1'], 'L0_gnn_ln2_w0': _L0_gnn_in['ln2_w0'], 'L0_gnn_ln2_b0': _L0_gnn_in['ln2_b0'], 'L0_gnn_ln2_w1': _L0_gnn_in['ln2_w1'], 'L0_gnn_msrc_ws': _L0_gnn_in['msrc_ws'], 'L0_gnn_msrc_wv': _L0_gnn_in['msrc_wv'], 'L0_gnn_mdst_ws': _L0_gnn_in['mdst_ws'], 'L0_gnn_mdst_bs': _L0_gnn_in['mdst_bs'], 'L0_gnn_mdst_wv': _L0_gnn_in['mdst_wv'], 'L0_gnn_rw1': _L0_gnn_in['rw1'], 'L0_gnn_rb1': _L0_gnn_in['rb1'], 'L0_gnn_rg1': _L0_gnn_in['rg1'], 'L0_gnn_rbe1': _L0_gnn_in['rbe1'], 'L0_gnn_rw2': _L0_gnn_in['rw2'], 'L0_gnn_rb2': _L0_gnn_in['rb2'], 'L0_gnn_rg2': _L0_gnn_in['rg2'], 'L0_gnn_rbe2': _L0_gnn_in['rbe2'], 'L0_gnn_rw3': _L0_gnn_in['rw3'], 'L0_gnn_roff': _L0_gnn_in['roff'], 'L0_gnn_lin_ws': _L0_gnn_in['lin_ws'], 'L0_gnn_lin_bs': _L0_gnn_in['lin_bs'], 'L0_gnn_lin_wv': _L0_gnn_in['lin_wv'], 'L0_gnn_alpha_dot': _L0_gnn_in['alpha_dot'], 'L0_gnn_proj_ws': _L0_gnn_in['proj_ws'], 'L0_gnn_proj_bs': _L0_gnn_in['proj_bs'], 'L0_gnn_proj_wv': _L0_gnn_in['proj_wv'], 'L0_gnn_f1_ws': _L0_gnn_in['f1_ws'], 'L0_gnn_f1_bs': _L0_gnn_in['f1_bs'], 'L0_gnn_f1_wv': _L0_gnn_in['f1_wv'], 'L0_gnn_f2_ws': _L0_gnn_in['f2_ws'], 'L0_gnn_f2_bs': _L0_gnn_in['f2_bs'], 'L0_gnn_f2_wv': _L0_gnn_in['f2_wv'], 'L1_gnn_lin1_ws': _L1_gnn_in['lin1_ws'], 'L1_gnn_lin1_wv': _L1_gnn_in['lin1_wv'], 'L1_gnn_fc_w1': _L1_gnn_in['fc_w1'], 'L1_gnn_fc_w2': _L1_gnn_in['fc_w2'], 'L1_gnn_sc_ws': _L1_gnn_in['sc_ws'], 'L1_gnn_sc_wv': _L1_gnn_in['sc_wv'], 'L1_gnn_lin2_ws': _L1_gnn_in['lin2_ws'], 'L1_gnn_lin2_wv': _L1_gnn_in['lin2_wv']}

def reference(x, src, dst, edge_attr_3, edge_attr_4, edge_attr_64, node_vec1, L0_gnn_ln1_w0, L0_gnn_ln1_b0, L0_gnn_ln1_w1, L0_gnn_ln2_w0, L0_gnn_ln2_b0, L0_gnn_ln2_w1, L0_gnn_msrc_ws, L0_gnn_msrc_wv, L0_gnn_mdst_ws, L0_gnn_mdst_bs, L0_gnn_mdst_wv, L0_gnn_rw1, L0_gnn_rb1, L0_gnn_rg1, L0_gnn_rbe1, L0_gnn_rw2, L0_gnn_rb2, L0_gnn_rg2, L0_gnn_rbe2, L0_gnn_rw3, L0_gnn_roff, L0_gnn_lin_ws, L0_gnn_lin_bs, L0_gnn_lin_wv, L0_gnn_alpha_dot, L0_gnn_proj_ws, L0_gnn_proj_bs, L0_gnn_proj_wv, L0_gnn_f1_ws, L0_gnn_f1_bs, L0_gnn_f1_wv, L0_gnn_f2_ws, L0_gnn_f2_bs, L0_gnn_f2_wv, L1_gnn_lin1_ws, L1_gnn_lin1_wv, L1_gnn_fc_w1, L1_gnn_fc_w2, L1_gnn_sc_ws, L1_gnn_sc_wv, L1_gnn_lin2_ws, L1_gnn_lin2_wv):
    import jax
    import jax.numpy as jnp

    def _L0_gnn_ref(node_input, node_attr, edge_vec, edge_scalars, edge_src, edge_dst, ln1_w0, ln1_b0, ln1_w1, ln2_w0, ln2_b0, ln2_w1, msrc_ws, msrc_wv, mdst_ws, mdst_bs, mdst_wv, rw1, rb1, rg1, rbe1, rw2, rb2, rg2, rbe2, rw3, roff, lin_ws, lin_bs, lin_wv, alpha_dot, proj_ws, proj_bs, proj_wv, f1_ws, f1_bs, f1_wv, f2_ws, f2_bs, f2_wv):
        import jax, jax.numpy as jnp
        import numpy as np
        N, E = (1250, 20000)
        C0, C1 = (64, 32)
        H, A = (8, 8)
        H0, H1 = (8, 4)
        M0, M1 = (128, 64)
        NG, RH = (64, 64)
        WN = C0 + C0 + C1 + C1 + C1
        DS, DV = (C0 + C1, C0 + 2 * C1)
        EPS = 1e-05
        SQ3 = np.float32(np.sqrt(3.0))
        SQ2 = np.float32(np.sqrt(2.0))

        def _split(x):
            return (x[:, :C0], x[:, C0:].reshape(x.shape[0], C1, 3))

        def _merge(s, v):
            return jnp.concatenate([s, v.reshape(v.shape[0], -1)], axis=1)

        def _eq_ln(x, w0, b0, w1):
            s, v = _split(x)
            s = s - s.mean(axis=1, keepdims=True)
            s = s * jax.lax.rsqrt(jnp.square(s).mean(axis=1, keepdims=True) + EPS) * w0 + b0
            v = v * jax.lax.rsqrt(jnp.square(v).mean(axis=(1, 2), keepdims=True) + EPS) * w1[None, :, None]
            return (s, v)

        def _eq_lin(s, v, ws, bs, wv):
            return (s @ ws + bs, jnp.einsum('nud,uk->nkd', v, wv))

        def _ln(x, g, b):
            xc = x - x.mean(-1, keepdims=True)
            return xc * jax.lax.rsqrt(jnp.square(xc).mean(-1, keepdims=True) + EPS) * g + b

        def _smooth_leaky(x, alpha=0.2):
            return 0.5 * (1 + alpha) * x + 0.5 * (1 - alpha) * x * (2.0 * jax.nn.sigmoid(x) - 1.0)

        def _forward(node_input, node_attr, edge_vec, edge_scalars, edge_src, edge_dst, ln1_w0, ln1_b0, ln1_w1, ln2_w0, ln2_b0, ln2_w1, msrc_ws, msrc_wv, mdst_ws, mdst_bs, mdst_wv, rw1, rb1, rg1, rbe1, rw2, rb2, rg2, rbe2, rw3, roff, lin_ws, lin_bs, lin_wv, alpha_dot, proj_ws, proj_bs, proj_wv, f1_ws, f1_bs, f1_wv, f2_ws, f2_bs, f2_wv):
            n = node_input.shape[0]
            s, v = _eq_ln(node_input, ln1_w0, ln1_b0, ln1_w1)
            src_s = s @ msrc_ws
            src_v = jnp.einsum('nud,uk->nkd', v, msrc_wv)
            dst_s = s @ mdst_ws + mdst_bs
            dst_v = jnp.einsum('nud,uk->nkd', v, mdst_wv)
            ms = src_s[edge_src] + dst_s[edge_dst]
            mv = src_v[edge_src] + dst_v[edge_dst]
            h = jax.nn.silu(_ln(edge_scalars @ rw1 + rb1, rg1, rbe1))
            h = jax.nn.silu(_ln(h @ rw2 + rb2, rg2, rbe2))
            w = h @ rw3 + roff
            rhat = edge_vec * jax.lax.rsqrt(jnp.sum(jnp.square(edge_vec), -1, keepdims=True) + 1e-12)
            Y1 = SQ3 * rhat
            w1, w2, w3, w4, w5 = jnp.split(w, [C0, 2 * C0, 2 * C0 + C1, 2 * C0 + 2 * C1], axis=1)
            o0a = w1 * ms
            o0b = w4 * (jnp.einsum('eud,ed->eu', mv, Y1) / SQ3)
            o1a = (w2 * ms)[:, :, None] * Y1[:, None, :]
            o1b = w3[:, :, None] * mv
            o1c = w5[:, :, None] * (jnp.cross(mv, Y1[:, None, :]) / SQ2)
            ds = jnp.concatenate([o0a, o0b], axis=1)
            dv = jnp.concatenate([o1a, o1b, o1c], axis=1)
            ls, lv = _eq_lin(ds, dv, lin_ws, lin_bs, lin_wv)
            e = ls.shape[0]
            alpha = ls[:, :H * A].reshape(e, H, A)
            vs = ls[:, H * A:].reshape(e, H, H0)
            vv = lv.reshape(e, H, H1, 3)
            a = jnp.einsum('ehk,hk->eh', _smooth_leaky(alpha), alpha_dot)
            amax = jax.lax.stop_gradient(jax.ops.segment_max(a, edge_dst, num_segments=n))
            a = jnp.exp(a - amax[edge_dst])
            a = a / (jax.ops.segment_sum(a, edge_dst, num_segments=n)[edge_dst] + 1e-12)
            ns = jax.ops.segment_sum(vs * a[..., None], edge_dst, num_segments=n).reshape(n, H * H0)
            nv = jax.ops.segment_sum(vv * a[..., None, None], edge_dst, num_segments=n).reshape(n, H * H1, 3)
            ps, pv = _eq_lin(ns, nv, proj_ws, proj_bs, proj_wv)
            x = node_input + _merge(ps, pv)
            s2, v2 = _eq_ln(x, ln2_w0, ln2_b0, ln2_w1)
            a0 = node_attr[:, :1]
            fs, fv = _eq_lin(s2, v2, f1_ws, f1_bs, f1_wv)
            fs = fs * a0
            fv = fv * a0[:, :, None]
            sc = jax.nn.silu(fs[:, :M0])
            fv = fv * jax.nn.sigmoid(fs[:, M0:])[:, :, None]
            os_, ov = _eq_lin(sc, fv, f2_ws, f2_bs, f2_wv)
            os_ = os_ * a0
            ov = ov * a0[:, :, None]
            return x + _merge(os_, ov)
        return _forward(node_input, node_attr, edge_vec, edge_scalars, edge_src, edge_dst, ln1_w0, ln1_b0, ln1_w1, ln2_w0, ln2_b0, ln2_w1, msrc_ws, msrc_wv, mdst_ws, mdst_bs, mdst_wv, rw1, rb1, rg1, rbe1, rw2, rb2, rg2, rbe2, rw3, roff, lin_ws, lin_bs, lin_wv, alpha_dot, proj_ws, proj_bs, proj_wv, f1_ws, f1_bs, f1_wv, f2_ws, f2_bs, f2_wv)

    def _L1_gnn_ref(node_features, node_attr, edge_src, edge_dst, edge_attr, edge_scalars, lin1_ws, lin1_wv, fc_w1, fc_w2, sc_ws, sc_wv, lin2_ws, lin2_wv):
        import jax, jax.numpy as jnp
        import numpy as np
        N, E = (5000, 80000)
        S_IN, V_IN = (64, 32)
        S_MID, V_MID = (96, 128)
        S_OUT, V_OUT = (96, 32)
        R = 64
        FC_HID = 64
        W_NUMEL = 64 + 64 + 32 + 32 + 32
        NUM_NEIGHBORS = 16.0

        def _inv(d):
            return 1.0 / jnp.sqrt(jnp.float32(d))

        def _forward(node_features, node_attr, edge_attr, edge_scalars, lin1_ws, lin1_wv, fc_w1, fc_w2, sc_ws, sc_wv, lin2_ws, lin2_wv, edge_src, edge_dst):
            n = node_features.shape[0]
            s = node_features[:, :S_IN]
            v = node_features[:, S_IN:].reshape(n, V_IN, 3)
            a = node_attr
            sc_s = s @ sc_ws * a * _inv(S_IN)
            sc_v = jnp.einsum('nci,cd->ndi', v, sc_wv) * a[:, :, None] * _inv(V_IN)
            h_s = s @ lin1_ws * a * _inv(S_IN)
            h_v = jnp.einsum('nci,cd->ndi', v, lin1_wv) * a[:, :, None] * _inv(V_IN)
            hid = jax.nn.silu(edge_scalars @ fc_w1 * _inv(R))
            w = hid @ fc_w2 * _inv(FC_HID)
            w1, w2, w3, w4, w5 = jnp.split(w, [64, 128, 160, 192], axis=-1)
            es = h_s[edge_src]
            ev = h_v[edge_src]
            e0 = edge_attr[:, :1]
            e1 = edge_attr[:, 1:4]
            m_s1 = w1 * es * e0
            m_s2 = w4 * jnp.einsum('eci,ei->ec', ev, e1) * _inv(3)
            m_v1 = (w2 * es)[:, :, None] * e1[:, None, :]
            m_v2 = w3[:, :, None] * ev * e0[:, :, None]
            m_v3 = w5[:, :, None] * jnp.cross(ev, e1[:, None, :]) * _inv(2)
            mid_s = jnp.concatenate([m_s1, m_s2], axis=-1)
            mid_v = jnp.concatenate([m_v1, m_v2, m_v3], axis=1)
            inv_nn = 1.0 / jnp.sqrt(jnp.float32(NUM_NEIGHBORS))
            agg_s = jax.ops.segment_sum(mid_s, edge_dst, num_segments=n) * inv_nn
            agg_v = jax.ops.segment_sum(mid_v, edge_dst, num_segments=n) * inv_nn
            o_s = agg_s @ lin2_ws * a * _inv(S_MID)
            o_v = jnp.einsum('nci,cd->ndi', agg_v, lin2_wv) * a[:, :, None] * _inv(V_MID)
            pre_s = sc_s + o_s
            pre_v = sc_v + o_v
            scalars = jax.nn.silu(pre_s[:, :64])
            gates = jax.nn.sigmoid(pre_s[:, 64:96])
            gated = gates[:, :, None] * pre_v
            return jnp.concatenate([scalars, gated.reshape(n, 3 * V_OUT)], axis=-1)
        return _forward(node_features, node_attr, edge_attr, edge_scalars, lin1_ws, lin1_wv, fc_w1, fc_w2, sc_ws, sc_wv, lin2_ws, lin2_wv, edge_src, edge_dst)
    x = _layernorm(x + _L0_gnn_ref(x, node_vec1, edge_attr_3, edge_attr_64, src, dst, L0_gnn_ln1_w0, L0_gnn_ln1_b0, L0_gnn_ln1_w1, L0_gnn_ln2_w0, L0_gnn_ln2_b0, L0_gnn_ln2_w1, L0_gnn_msrc_ws, L0_gnn_msrc_wv, L0_gnn_mdst_ws, L0_gnn_mdst_bs, L0_gnn_mdst_wv, L0_gnn_rw1, L0_gnn_rb1, L0_gnn_rg1, L0_gnn_rbe1, L0_gnn_rw2, L0_gnn_rb2, L0_gnn_rg2, L0_gnn_rbe2, L0_gnn_rw3, L0_gnn_roff, L0_gnn_lin_ws, L0_gnn_lin_bs, L0_gnn_lin_wv, L0_gnn_alpha_dot, L0_gnn_proj_ws, L0_gnn_proj_bs, L0_gnn_proj_wv, L0_gnn_f1_ws, L0_gnn_f1_bs, L0_gnn_f1_wv, L0_gnn_f2_ws, L0_gnn_f2_bs, L0_gnn_f2_wv), axis=-1)
    x = _layernorm(x + _L1_gnn_ref(x, node_vec1, src, dst, edge_attr_4, edge_attr_64, L1_gnn_lin1_ws, L1_gnn_lin1_wv, L1_gnn_fc_w1, L1_gnn_fc_w2, L1_gnn_sc_ws, L1_gnn_sc_wv, L1_gnn_lin2_ws, L1_gnn_lin2_wv), axis=-1)
    return x

_drawn_inputs = setup_inputs


def setup_inputs(seed=0):
    import zlib

    import numpy as np

    out = dict(_drawn_inputs(seed))
    spreads = {'L0_gnn_ln1_w0': (1.0, 0.2),
     'L0_gnn_ln1_b0': (0.0, 0.383),
     'L0_gnn_ln1_w1': (1.0, 0.6),
     'L0_gnn_ln2_w0': (1.0, 0.6),
     'L0_gnn_ln2_b0': (0.0, 0.8),
     'L0_gnn_ln2_w1': (1.0, 0.6),
     'L0_gnn_mdst_bs': (0.0, 0.529),
     'L0_gnn_rb1': (0.0, 0.1),
     'L0_gnn_rg1': (1.0, 0.2),
     'L0_gnn_rbe1': (0.0, 0.302),
     'L0_gnn_rb2': (0.0, 0.1),
     'L0_gnn_rg2': (1.0, 0.2),
     'L0_gnn_rbe2': (0.0, 0.315),
     'L0_gnn_lin_bs': (0.0, 0.281),
     'L0_gnn_proj_bs': (0.0, 0.268),
     'L0_gnn_f1_bs': (0.0, 0.8),
     'L0_gnn_f2_bs': (0.0, 0.504)}
    factors = {}
    for name, (base, spread) in spreads.items():
        noise = np.random.default_rng([zlib.crc32(name.encode()), seed]).standard_normal(out[name].shape)
        drawn = base * np.exp(spread * noise) if base else spread * noise
        out[name] = jnp.asarray(drawn.astype(out[name].dtype))
    for name, factor in factors.items():
        out[name] = (out[name] * factor).astype(out[name].dtype)
    return out
```

```python
from contextlib import ExitStack

import numpy as np

import concourse.bass as bass
from concourse import mybir

F32 = mybir.dt.float32
I32 = mybir.dt.int32
BF16 = mybir.dt.bfloat16
ALU = mybir.AluOpType
ACT = mybir.ActivationFunctionType
AX = mybir.AxisListType

P = 128
Q = 32
NODES, EDGES = 12500, 212500
S, V, D = 64, 32, 3
VD = V * D
FEAT = S + VD
HEADS = 8
WN = 2 * S + 3 * V
TILES = -(-EDGES // P)
BLOCKS = -(-NODES // P)
UNIT = 4
ITER = 2 * UNIT
ITERS = -(-(TILES + BLOCKS - 1) // ITER)
STEPS = ITERS * ITER
STEP_COLS = -(-(STEPS + 2 * ITER) // P)
TABLE = STEP_COLS * P
NB = 7
NODE_ITERS = BLOCKS // NB
assert NODE_ITERS * NB == BLOCKS
EPS = 1e-5
BIG = 1e30
TABLES = "natural_log_exp_and_others"
KEYED = HEADS + 1
MSG = FEAT + HEADS
CHAN = 2 * S + VD + V + VD


def bc(ap, axis, n):
    a = ap.unsqueeze(axis)
    shape = list(a.shape)
    shape[axis] = n
    return a.broadcast_to(shape)


class Arena:

    def __init__(self, nc, ctx, tag):
        self.nc, self.ctx, self.tag = nc, ctx, tag
        self.sems = []
        ctx.callback(self.clear)

    def sb(self, name, shape, dt=F32):
        return self.ctx.enter_context(self.nc.sbuf_tensor(f"{self.tag}_{name}", shape, dt))

    def banks(self):
        return self.ctx.enter_context(self.nc.psum_tensor(f"{self.tag}_banks", [P, 8, 512], F32))

    def sem(self, name):
        self.sems.append(self.nc.alloc_semaphore(f"{self.tag}_{name}"))
        return self.sems[-1]

    def clear(self):
        self.nc.clear_and_free_semaphores(self.sems)
        self.nc.all_engine_barrier()


class Chain:

    def __init__(self, engine, sem, turn=0, per=0):
        self.engine, self.sem, self.base, self.n, self.per = engine, sem, turn * per, 0, per

    def link(self, ins):
        self.n += 1
        ins.then_inc(self.sem, 1)
        self.engine.wait_ge(self.sem, self.base + self.n)

    def close(self):
        assert self.n == self.per, (self.n, self.per)


def hold(engine, passed, *waits):
    for s, value in waits:
        engine.wait_ge(s, value)
    engine.sem_inc(passed, 1)


def load_kron(eng, done, dst, row, col, w):
    k, m = w.shape
    for d in range(D):
        eng.dma_start(dst[row + d:row + D * k:D, col + d:col + D * m:D], w,
                      allow_slow_non_contiguous=True).then_inc(done, 16)
    return D * 16


def row_of(v):
    return v.rearrange("(a n) -> a n", a=1)


def col_of(v):
    return v.rearrange("(n a) -> n a", a=1)


def spread(v, n=P):
    return row_of(v).broadcast_to([n, v.shape[0]])


def phase_steps(nc, dst_first, dst_last, step_tile, step_block, step_base):
    with ExitStack() as ctx:
        a = Arena(nc, ctx, "steps")
        di = a.sb("di", [P, 2, TILES], I32)
        bi = a.sb("bi", [P, 2, TILES], I32)
        bf = a.sb("bf", [P, 2, TILES])
        count = a.sb("count", [P, TILES])
        upto = a.sb("upto", [P, TILES])
        start = a.sb("start", [P, TILES])
        shift = a.sb("shift", [P, TILES])
        dshift = a.sb("dshift", [P, TILES])
        ones = a.sb("ones", [P, TILES])
        junk = a.sb("junk", [P, 2, TILES])
        si = a.sb("si", [P, STEP_COLS], I32)
        sf = a.sb("sf", [P, STEP_COLS])
        acc = a.sb("acc", [P, 2, STEP_COLS])
        tf = a.sb("tf", [P, 3, STEP_COLS])
        ti = a.sb("ti", [P, 2, STEP_COLS], I32)
        loaded, numbered, counted, table_done, stored = (
            a.sem(n) for n in ("loaded", "numbered", "counted", "table_done", "stored"))
        with nc.Block() as block:
            @block.sync
            def _(sp):
                sp.dma_start(di[:, 0, :], spread(dst_first)).then_inc(loaded, 16)
                sp.dma_start(di[:, 1, :], spread(dst_last)).then_inc(loaded, 16)
                sp.wait_ge(table_done, 1)
                for n, where in enumerate((step_tile, step_block)):
                    sp.dma_start(where.rearrange("(c p) -> p c", p=P), ti[:, n, :],
                                 allow_slow_non_contiguous=True).then_inc(stored, 16)
                sp.dma_start(step_base.rearrange("(c p) -> p c", p=P), tf[:, 2, :],
                             allow_slow_non_contiguous=True).then_inc(stored, 16)
                sp.wait_ge(stored, 48)

            @block.gpsimd
            def _(pool):
                nc.gpsimd.iota(si[:, :], pattern=[[P, STEP_COLS]], base=0, channel_multiplier=1).then_inc(numbered, 1)

            @block.vector
            def _(dve):
                v = nc.vector
                c = Chain(dve, counted)
                v.memset(ones[:, :], 1.0)
                dve.wait_ge(loaded, 32)
                c.link(v.tensor_scalar(bi[:, :, :], di[:, :, :], 7, None, ALU.arith_shift_right))
                c.link(v.tensor_copy(bf[:, :, :], bi[:, :, :]))
                c.link(v.scalar_tensor_tensor(count[:, :], bf[:, 1, :], 1.0, bf[:, 0, :], ALU.add, ALU.subtract))
                c.link(v.tensor_tensor_scan(upto[:, :], ones[:, :], count[:, :], 0.0, ALU.mult, ALU.add))
                c.link(v.tensor_tensor(start[:, :], upto[:, :], count[:, :], ALU.subtract))
                c.link(v.tensor_tensor(shift[:, :], bf[:, 0, :], start[:, :], ALU.subtract))
                v.tensor_copy(dshift[:, 0:1], shift[:, 0:1])
                c.link(v.tensor_tensor(dshift[:, 1:], shift[:, 1:], shift[:, :TILES - 1], ALU.subtract))
                dve.wait_ge(numbered, 1)
                c.link(v.tensor_copy(sf[:, :], si[:, :]))
                for col in range(STEP_COLS):
                    for n, what in enumerate((ones, dshift)):
                        c.link(v.scalar_tensor_tensor(junk[:, n, :], start[:, :], sf[:, col:col + 1], what[:, :],
                                                      ALU.is_le, ALU.mult, accum_out=acc[:, n, col:col + 1]))
                c.link(v.tensor_scalar(tf[:, 0, :], acc[:, 0, :], -1.0, None, ALU.add))
                c.link(v.tensor_tensor(tf[:, 1, :], acc[:, 1, :], sf[:, :], ALU.add))
                c.link(v.tensor_scalar(tf[:, 1, :], tf[:, 1, :], float(BLOCKS), None, ALU.min))
                c.link(v.tensor_scalar(tf[:, 2, :], tf[:, 1, :], float(P), None, ALU.mult))
                v.tensor_copy(ti[:, :, :], tf[:, 0:2, :]).then_inc(table_done, 1)


def eq_norm_sums(v, c, x, mu, cs, sq, stat):
    c.link(v.tensor_reduce(mu[:, :], x[:, :, 0:S], AX.X, ALU.add))
    c.link(v.tensor_scalar(mu[:, :], mu[:, :], -1.0 / S, None, ALU.mult))
    c.link(v.tensor_tensor(cs[:, :, 0:S], x[:, :, 0:S], bc(mu[:, :], 2, S), ALU.add))
    v.tensor_tensor(sq[:, :, 0:S], cs[:, :, 0:S], cs[:, :, 0:S], ALU.mult)
    c.link(v.tensor_tensor(sq[:, :, S:FEAT], x[:, :, S:FEAT], x[:, :, S:FEAT], ALU.mult))
    v.tensor_reduce(stat[:, 0, :], sq[:, :, 0:S], AX.X, ALU.add)
    c.link(v.tensor_reduce(stat[:, 1, :], sq[:, :, S:FEAT], AX.X, ALU.add))
    v.tensor_scalar(stat[:, 0, :], stat[:, 0, :], 1.0 / S, EPS, ALU.mult, ALU.add)
    return v.tensor_scalar(stat[:, 1, :], stat[:, 1, :], 1.0 / VD, EPS, ALU.mult, ALU.add)


def eq_norm_apply(v, c, x, cs, stat, xn):
    v.tensor_tensor(xn[:, :, 0:S], cs[:, :, 0:S], bc(stat[:, 0, :], 2, S), ALU.mult)
    return v.tensor_tensor(xn[:, :, S:FEAT], x[:, :, S:FEAT], bc(stat[:, 1, :], 2, VD), ALU.mult)


def inverse_root(s, c, stat, log):
    c.link(s.activation(log, stat, ACT.Ln))
    return s.activation(stat, log, ACT.Exp, scale=-0.5)


def full_norm_sums(v, c, x, mu, cs, sq, stat):
    c.link(v.tensor_reduce(mu[:, :], x[:, :, :], AX.X, ALU.add))
    c.link(v.tensor_scalar(mu[:, :], mu[:, :], -1.0 / FEAT, None, ALU.mult))
    c.link(v.tensor_tensor(cs[:, :, :], x[:, :, :], bc(mu[:, :], 2, FEAT), ALU.add))
    c.link(v.tensor_tensor(sq[:, :, :], cs[:, :, :], cs[:, :, :], ALU.mult))
    c.link(v.tensor_reduce(stat[:, 0, :], sq[:, :, :], AX.X, ALU.add))
    return v.tensor_scalar(stat[:, 0, :], stat[:, 0, :], 1.0 / FEAT, EPS, ALU.mult, ALU.add)


def turn_features(t, banks, src, ident):
    for b in range(NB):
        cols = slice(b % 4 * P, b % 4 * P + P)
        t.transpose(banks[0:VD, 2 + b // 4, cols], src[:, b, S:FEAT], ident[:, :])
        last = t.transpose(banks[0:S, b // 4, cols], src[:, b, 0:S], ident[:, :])
    return last


def turned(banks, rows, first):
    for n, cols in enumerate((4 * P, (NB - 4) * P)):
        yield banks[0:rows, first + n, 0:cols], slice(n * 4 * P, n * 4 * P + cols)


def make_identity(nc, pool, ident, cleared, ready):
    nc.gpsimd.memset(ident[:, :], 0.0).then_inc(cleared, 1)
    pool.wait_ge(cleared, 1)
    nc.gpsimd.affine_select(out=ident[:, :], in_=ident[:, :], compare_op=ALU.not_equal, fill=1.0, base=0,
                            pattern=[[-1, P]], channel_multiplier=1).then_inc(ready, 1)


def phase_nodes_in(nc, x, w, src_table, dst_feat):
    with ExitStack() as ctx:
        a = Arena(nc, ctx, "nin")
        banks = a.banks()
        ident = a.sb("ident", [P, P])
        w_s = a.sb("w_s", [S, 2 * S])
        w_v = a.sb("w_v", [VD, 2 * VD])
        bias = a.sb("bias", [P, S])
        g_s, b_s = a.sb("g_s", [S, 1]), a.sb("b_s", [S, 1])
        g_v = a.sb("g_v", [VD, 1])
        xb = a.sb("xb", [P, NB, FEAT])
        cs = a.sb("cs", [P, NB, FEAT])
        sq = a.sb("sq", [P, NB, FEAT])
        xn = a.sb("xn", [P, NB, FEAT])
        mu = a.sb("mu", [P, NB])
        stat = a.sb("stat", [P, 2, NB])
        log = a.sb("log", [P, 2, NB])
        sT = a.sb("sT", [S, NB * P])
        vT = a.sb("vT", [VD, NB * P])
        out = a.sb("out", [P, NB, FEAT])
        (cleared, ident_ready, zeroed, weights, x_ready, summed, rooted, normed, turned_pe, turned_sb, mapped,
         dst_kept, src_kept, stored, dve_chain, act_chain, sp_passed) = (a.sem(n) for n in (
             "cleared", "ident_ready", "zeroed", "weights", "x_ready", "summed", "rooted", "normed", "turned_pe",
             "turned_sb", "mapped", "dst_kept", "src_kept", "stored", "dve_chain", "act_chain", "sp_passed"))
        xr = x.rearrange("(i j p) f -> i p j f", j=NB, p=P)
        tr = src_table.rearrange("(i j p) f -> i p j f", j=NB, p=P)
        with nc.Block() as block:
            @block.gpsimd
            def _(pool):
                make_identity(nc, pool, ident, cleared, ident_ready)
                nc.gpsimd.memset(w_v[:, :], 0.0).then_inc(zeroed, 1)

            @block.sync
            def _(sp):
                n = 0
                for dst, src in ((w_s[:, 0:S], w["msrc_ws"]), (w_s[:, S:], w["mdst_ws"]), (bias[:, :], spread(w["mdst_bs"])),
                                 (g_s[:, :], col_of(w["ln1_w0"])), (b_s[:, :], col_of(w["ln1_b0"]))):
                    sp.dma_start(dst, src).then_inc(weights, 16)
                    n += 16
                for d in range(D):
                    sp.dma_start(g_v[d:VD:D, :], col_of(w["ln1_w1"])).then_inc(weights, 16)
                    n += 16
                sp.wait_ge(zeroed, 1)
                n += load_kron(sp, weights, w_v, 0, 0, w["msrc_wv"])
                n += load_kron(sp, weights, w_v, 0, VD, w["mdst_wv"])
                sp.wait_ge(weights, n)
                with sp.Fori(0, NODE_ITERS) as i:
                    sp.dma_start(xb[:, :, :], xr[i]).then_inc(x_ready, 16)
                    hold(sp, sp_passed, (src_kept, i + 1))
                    sp.dma_start(tr[i], out[:, :, :]).then_inc(stored, 16)
                    hold(sp, sp_passed, (stored, 16 * i + 16))

            @block.vector
            def _(dve):
                v = nc.vector
                v.memset(dst_feat[:, BLOCKS, :], 0.0)
                with dve.Fori(0, NODE_ITERS) as i:
                    c = Chain(dve, dve_chain, i, 5)
                    dve.wait_ge(x_ready, 16 * i + 16)
                    eq_norm_sums(v, c, xb, mu, cs, sq, stat).then_inc(summed, 1)
                    c.close()
                    dve.wait_ge(rooted, i + 1)
                    eq_norm_apply(v, c, xb, cs, stat, xn).then_inc(normed, 1)
                    dve.wait_ge(mapped, i + 1)
                    for b in range(NB):
                        p = banks[:, (4 + b) % 8, :]
                        v.tensor_tensor(dst_feat[:, bass.ds(i * NB + b, 1), 0:S].rearrange("p a f -> p (a f)"),
                                        p[:, S:2 * S], bias[:, :], ALU.add)
                        last = v.tensor_copy(dst_feat[:, bass.ds(i * NB + b, 1), S:FEAT].rearrange("p a f -> p (a f)"),
                                             p[:, 2 * S + VD:2 * FEAT])
                    last.then_inc(dst_kept, 1)

            @block.scalar
            def _(act):
                s = nc.scalar
                s.preload_act_table_set(TABLES)
                with act.Fori(0, NODE_ITERS) as i:
                    c = Chain(act, act_chain, i, 1)
                    act.wait_ge(summed, i + 1)
                    inverse_root(s, c, stat[:, :, :], log[:, :, :]).then_inc(rooted, 1)
                    act.wait_ge(turned_pe, i + 1)
                    for p, cols in turned(banks, S, 0):
                        s.activation(sT[:, cols], p, ACT.Identity, bias=b_s[:, :], scale=g_s[:, :])
                    for p, cols in turned(banks, VD, 2):
                        last = s.activation(vT[:, cols], p, ACT.Identity, scale=g_v[:, :])
                    last.then_inc(turned_sb, 1)
                    act.wait_ge(dst_kept, i + 1)
                    for b in range(NB):
                        p = banks[:, (4 + b) % 8, :]
                        s.activation(out[:, b, 0:S], p[:, 0:S], ACT.Copy)
                        last = s.activation(out[:, b, S:FEAT], p[:, 2 * S:2 * S + VD], ACT.Copy)
                    last.then_inc(src_kept, 1)

            @block.tensor
            def _(pe):
                t = nc.tensor
                pe.wait_ge(ident_ready, 1)
                pe.wait_ge(weights, 16 * (8 + 2 * D))
                with pe.Fori(0, NODE_ITERS) as i:
                    pe.wait_ge(normed, i + 1)
                    turn_features(t, banks, xn, ident).then_inc(turned_pe, 1)
                    pe.wait_ge(turned_sb, i + 1)
                    for b in range(NB):
                        p = banks[:, (4 + b) % 8, :]
                        cols = slice(b * P, b * P + P)
                        t.matmul(p[:, 0:2 * S], sT[:, cols], w_s[:, :], start=True, stop=True)
                        last = t.matmul(p[:, 2 * S:2 * FEAT], vT[:, cols], w_v[:, :], start=True, stop=True)
                    last.then_inc(mapped, 1)


def phase_edges(nc, attention, x_table, esT, src_dst, geometry, step_tile, step_block, step_base, w,
                dst_feat=None, messages=None, keyed=None, sums=None):
    g_cols = D if attention else D + 1
    ls = 2 * S if attention else S + V
    mcols = FEAT if attention else S + V + VD
    norms = 2 if attention else 0
    layers = 2 if attention else 1
    OUT_A, OUT_S, OUT_V = 0, V, V + ls
    C3 = 2 * S
    C4, C5 = C3 + VD, C3 + VD + V
    with ExitStack() as ctx:
        a = Arena(nc, ctx, "att" if attention else "conv")
        banks = a.banks()
        BX, BV, BM, BW, BT, BL = 0, 1, 2, 3, 4, 6
        ident, number = a.sb("ident", [P, P]), a.sb("number", [P, P])
        net = [a.sb(f"net{n}", [P, P]) for n in range(layers)]
        mean = a.sb("mean", [P, P])
        w_last = a.sb("w_last", [P, WN])
        net_cols = a.sb("net_cols", [P, 2, 5])
        rowsum = a.sb("rowsum", [P, 2, 2])
        rb_rows, rb_mean = a.sb("rb_rows", [P, 2, S]), a.sb("rb_mean", [P, 2])
        w_a, w_b, w_c = a.sb("w_a", [P, V + ls]), a.sb("w_b", [P, ls + VD]), a.sb("w_c", [VD, VD])
        rows3 = a.sb("rows3", [3 * Q, 2, WN])
        bias3 = a.sb("bias3", [3 * Q, 2, WN], BF16)
        ones3 = a.sb("ones3", [3 * Q, P], BF16)
        adot = a.sb("adot", [P, S])
        base = a.sb("base", [P, TABLE])
        tiles_sb = a.sb("tiles_sb", [1, TABLE], I32)
        blocks_sb = a.sb("blocks_sb", [1, TABLE], I32)
        es = a.sb("es", [P, UNIT * P])
        sq, rs, xn, z, e = (a.sb(n, [P, UNIT * P]) for n in ("sq", "rs", "xn", "z", "e"))
        hid = [a.sb(f"hid{n}", [P, UNIT * P]) for n in range(layers)]
        idx = [a.sb(f"idx{h}", [P, UNIT, 2], I32) for h in range(2)]
        geo = [a.sb(f"geo{h}", [P, UNIT, g_cols]) for h in range(2)]
        src = [a.sb(f"src{h}", [P, UNIT, FEAT]) for h in range(2)]
        dstf, rel = a.sb("dstf", [P, UNIT]), a.sb("rel", [P, UNIT])
        valid = a.sb("valid", [P, 2, UNIT])
        onehot = [a.sb(f"onehot{h}", [P, UNIT * P]) for h in range(2)]
        onehotT = a.sb("onehotT", [P, UNIT * P])
        gsq = a.sb("gsq", [P, UNIT, D])
        glen, glog = [a.sb(f"glen{h}", [P, UNIT]) for h in range(2)], a.sb("glog", [P, UNIT])
        yx = [a.sb(f"yx{h}", [P, UNIT, 5]) for h in range(2)]
        m = a.sb("m", [P, UNIT, FEAT])
        wS = a.sb("wS", [P, UNIT, WN])
        p0, p1, p2 = (a.sb(n, [P, UNIT, V, D]) for n in ("p0", "p1", "p2"))
        dot = a.sb("dot", [P, UNIT, V])
        ch = [a.sb(f"ch{h}", [P, UNIT, CHAN]) for h in range(2)]
        chT = a.sb("chT", [P, 3, UNIT * P])
        ty = a.sb("ty", [P, UNIT, V, D])
        msg = [a.sb(f"msg{h}", [P, UNIT, mcols]) for h in range(2)]
        key = [a.sb(f"key{h}", [P, UNIT, KEYED]) for h in range(2)]
        dkey = [a.sb(f"dkey{h}", [P, UNIT]) for h in range(2)]
        ea, ra = a.sb("ea", [P, UNIT, S]), a.sb("ra", [P, UNIT, S])
        dummy = a.sb("dummy", [1, 2])

        names = ("cleared ident_ready zeroed weights prepared tables prep_chain es_landed x_done v_done sq_done "
                 "log_done rs_done xn_done z_done e_done u_done r_done h_done df_done rel_done oh_done "
                 "ohT_done oht_done val_done key_done gsq_done glen_done glog_done gr_done yx_done m_done madd_done w_done "
                 "wev_done p_done dot_done cross_done prod_done bt_done bev_done lin_done act_post ty_done "
                 "ea_done u2_done r2_done sl_done ad_done post_done agg_done acc_done first_ready sp_passed pool_passed").split()
        sem = {n: a.sem(n) for n in names}

        (cleared, ident_ready, zeroed, weights, prepared, tables, prep_chain, es_landed, x_done, v_done, sq_done,
         log_done, rs_done, xn_done, z_done, e_done, u_done, r_done, h_done, df_done, rel_done, oh_done,
         ohT_done, oht_done, val_done, key_done, gsq_done, glen_done, glog_done, gr_done, yx_done, m_done, madd_done, w_done,
         wev_done, p_done, dot_done, cross_done, prod_done, bt_done, bev_done, lin_done, act_post, ty_done,
         ea_done, u2_done, r2_done, sl_done, ad_done, post_done, agg_done, acc_done, first_ready, sp_passed, pool_passed) = (sem[n] for n in names)
        idx_landed = [a.sem(f"idx_landed{h}") for h in range(2)]
        geo_landed = [a.sem(f"geo_landed{h}") for h in range(2)]
        src_landed = [a.sem(f"src_landed{h}") for h in range(2)]
        msg_stored = [a.sem(f"msg_stored{h}") for h in range(2)]
        key_stored = [a.sem(f"key_stored{h}") for h in range(2)]
        n_weights = [0]

        def at_least(engine, s, value):
            if not (isinstance(value, int) and value <= 0):
                engine.wait_ge(s, value)

        with nc.Block() as block:
            @block.sync
            def _(sp):
                def load(dst, source, slow=False):
                    sp.dma_start(dst, source, allow_slow_non_contiguous=slow).then_inc(weights, 16)
                    n_weights[0] += 16

                sp.dma_start(tiles_sb[:, :], row_of(step_tile)).then_inc(tables, 16)
                sp.dma_start(blocks_sb[:, :], row_of(step_block)).then_inc(tables, 16)
                sp.dma_start(base[:, :], spread(step_base)).then_inc(tables, 16)
                if attention:
                    for h in range(2):
                        sp.dma_start(dummy[:, 0:1], row_of(step_base)[:, 0:1]).then_inc(msg_stored[h], 16)
                        sp.wait_ge(msg_stored[h], 16)
                        sp.dma_start(dummy[:, 0:1], row_of(step_base)[:, 0:1]).then_inc(key_stored[h], 16)
                        sp.wait_ge(key_stored[h], 16)
                sp.wait_ge(zeroed, 1)
                sp.wait_ge(prep_chain, layers)
                for h in range(2):
                    r = slice(h * S, h * S + S)
                    load(w_last[r, :], w["w_last"])
                    for n in range(layers):
                        load(net[n][r, r], w["net"][n])
                    if attention:
                        for n in range(2):
                            for col, name in enumerate(("rb", "rg", "rbe")):
                                load(net_cols[r, n, col:col + 1], col_of(w[name][n]))
                if attention:
                    for n in range(2):
                        load(rb_rows[:, n, :], spread(w["rb"][n]))
                load(w_a[0:S, V:V + ls], w["lin_ws"][0:S, :])
                load(w_a[S:2 * S, 0:V], w["lin_wv"][0:S, :])
                load(w_b[VD:P, 0:ls], w["lin_ws"][S:S + V, :])
                n_weights[0] += load_kron(sp, weights, w_b, 0, ls, w["lin_wv"][S:S + V, :])
                n_weights[0] += load_kron(sp, weights, w_c, 0, 0, w["lin_wv"][S + V:S + 2 * V, :])
                if attention:
                    for part in range(3):
                        load(rows3[part * Q:part * Q + 1, 0, :], row_of(w["roff"]))
                        load(rows3[part * Q:part * Q + 1, 1, 0:2 * S], row_of(w["lin_bs"]))
                    load(adot[:, :], w["adot"].rearrange("h k -> (h k)").rearrange("(a n) -> a n", a=1).broadcast_to([P, S]))
                sp.wait_ge(tables, 48)
                sp.wait_ge(weights, n_weights[0])
                sp.sem_inc(first_ready, 1)

                def tile_of(step):
                    return sp.value_load(tiles_sb[0:1, bass.ds(step, 1)], min_val=0, max_val=TILES - 1)

                def load_es(j):
                    for u in range(ITER):
                        t = tile_of(ITER * j + u)
                        sp.dma_start(es[u // UNIT * S:u // UNIT * S + S, u % UNIT * P:u % UNIT * P + P],
                                     esT[bass.ds(t, 1), :, :].rearrange("a r p -> (a r) p")).then_inc(es_landed, 16)

                def load_half(k, h, wait_idx, wait_geo):
                    ts = []
                    wait_idx()
                    for u in range(UNIT):
                        t = tile_of(UNIT * k + u)
                        sp.dma_start(idx[h][:, u, :], src_dst[bass.ds(t, 1), :, :].rearrange("a p c -> (a p) c"))\
                            .then_inc(idx_landed[h], 16)
                        ts.append(t)
                    wait_geo()
                    for u in range(UNIT):
                        sp.dma_start(geo[h][:, u, :], geometry[bass.ds(ts[u], 1), :, :].rearrange("a p c -> (a p) c"))\
                            .then_inc(geo_landed[h], 16)

                def store(k, h):
                    hold(sp, sp_passed, (post_done, k + 1))
                    sp.dma_start(messages[:, bass.ds(UNIT * k, UNIT), :], msg[h][:, :, :]).then_inc(msg_stored[h], 16)
                    sp.dma_start(keyed[:, bass.ds(UNIT * k, UNIT), :], key[h][:, :, :]).then_inc(key_stored[h], 16)

                nothing = lambda: None
                load_es(0)
                load_half(0, 0, nothing, nothing)
                load_half(1, 1, nothing, nothing)
                sp.wait_ge(x_done, 1)
                load_es(1)
                with sp.Fori(0, ITERS) as i:
                    for h in range(2):
                        k = 2 * i + 2 + h

                        def wait_idx():
                            hold(sp, sp_passed, (oh_done, k - 1), (src_landed[h], 16 * UNIT * (i + 1)))
                        load_half(k, h, wait_idx, lambda: hold(sp, sp_passed, (prod_done, k - 1)))
                    if attention:
                        store(2 * i, 0)
                    hold(sp, sp_passed, (x_done, layers * (i + 1) + 1))
                    load_es(i + 2)
                    if attention:
                        store(2 * i + 1, 1)
                for h in range(2):
                    sp.wait_ge(idx_landed[h], 16 * UNIT * (ITERS + 1))
                    sp.wait_ge(geo_landed[h], 16 * UNIT * (ITERS + 1))
                    if attention:
                        sp.wait_ge(msg_stored[h], 16 * (ITERS + 1))
                        sp.wait_ge(key_stored[h], 16 * (ITERS + 1))
                sp.wait_ge(es_landed, 16 * ITER * (ITERS + 2))

            @block.gpsimd
            def _(pool):
                g = nc.gpsimd
                make_identity(nc, pool, ident, cleared, ident_ready)
                g.iota(number[:, :], pattern=[[1, P]], base=0, channel_multiplier=0,
                       allow_small_or_imprecise_dtypes=True)
                for t in (w_a, w_b, w_c):
                    g.memset(t[:, :], 0.0)
                g.memset(rows3[:, :, :], 0.0)
                g.memset(ones3[:, :], 1.0).then_inc(zeroed, 1)

                def gather(h, turn):
                    hold(pool, pool_passed, (idx_landed[h], 16 * UNIT * (turn + 1)))
                    for u in range(UNIT):
                        g.indirect_dma_start(out=src[h][:, u, :], out_offset=None, in_=x_table[:, :],
                                             in_offset=bass.IndirectOffsetOnAxis(ap=idx[h][:, u, 0:1], axis=0))\
                            .then_inc(src_landed[h], 16)

                gather(0, 0)
                gather(1, 0)
                with pool.Fori(0, ITERS) as i:
                    for h in range(2):
                        k = 2 * i + 2 + h
                        if attention:
                            pool.wait_ge(madd_done, 2 * (k - 1))
                        else:
                            pool.wait_ge(prod_done, k - 1)
                        gather(h, i + 1)
                for h in range(2):
                    pool.wait_ge(src_landed[h], 16 * UNIT * (ITERS + 1))

            @block.tensor
            def _(pe):
                t = nc.tensor

                def net_map(j, n):
                    if n == 0:
                        pe.wait_ge(es_landed, 16 * ITER * (j + 1))
                    else:
                        pe.wait_ge(h_done, layers * j + n)
                    t.matmul(banks[:, BX, :], net[n][:, :], (es if n == 0 else hid[n - 1])[:, :],
                             start=True, stop=True).then_inc(x_done, 1)

                def net_var(j, n):
                    pe.wait_ge(sq_done, layers * j + n + 1)
                    t.matmul(banks[:, BV, :], mean[:, :], sq[:, :], start=True, stop=True).then_inc(v_done, 1)

                def turn_onehot(k, h):
                    pe.wait_ge(oh_done, k + 1)
                    for u in range(UNIT):
                        last = t.transpose(banks[:, BT, u * P:u * P + P], onehot[h][:, u * P:u * P + P], ident[:, :])
                    last.then_inc(ohT_done, 1)

                def gather(k, pair):
                    if pair == 0:
                        pe.wait_ge(oht_done, k + 1)
                    at_least(pe, madd_done, 2 * k + pair)
                    for n in range(2):
                        u = 2 * pair + n
                        b = pe.value_load(blocks_sb[0:1, bass.ds(UNIT * k + u, 1)], min_val=0, max_val=BLOCKS)
                        last = t.matmul(banks[:, BM, n * FEAT:n * FEAT + FEAT], onehotT[:, u * P:u * P + P],
                                        dst_feat[:, bass.ds(b, 1), :].rearrange("p a f -> p (a f)"),
                                        start=True, stop=True)
                    last.then_inc(m_done, 1)

                def gather_and_weights(k, h, j, gathered=False):
                    for pair in range(2):
                        if attention and not (gathered and pair == 0):
                            gather(k, pair)
                        if pair == 0:
                            pe.wait_ge(h_done, layers * (j + 1))
                        at_least(pe, wev_done, 2 * k + pair)
                        for n in range(2):
                            u = 2 * pair + n
                            out = banks[:, BW, n * WN:n * WN + WN]
                            last = t.matmul(out, hid[-1][h * S:h * S + S, u * P:u * P + P], w_last[h * S:h * S + S, :],
                                            start=True, stop=not attention)
                            if attention:
                                last = t.matmul(out, ones3[:, :], bias3[:, 0, :], start=False, stop=True)
                        last.then_inc(w_done, 1)

                def turn_channels(k, h):
                    pe.wait_ge(prod_done, k + 1)
                    for c, (lo, hi) in enumerate(((0, P), (P, 2 * P), (2 * P, CHAN))):
                        if c == 0 and attention:
                            pe.wait_ge(oht_done, k + 2)
                        if c == 2:
                            pe.wait_ge(bev_done, 3 * k + 1)
                        for u in range(UNIT):
                            last = t.transpose(banks[0:hi - lo, BT + c % 2, u * P:u * P + P], ch[h][:, u, lo:hi], ident[:, :])
                        last.then_inc(bt_done, 1)

                def linear(k):
                    pe.wait_ge(bev_done, 3 * k + 3)
                    for u in range(UNIT):
                        out = banks[:, BL + u // 2, u % 2 * 256:u % 2 * 256 + 256]
                        cols = slice(u * P, u * P + P)
                        t.matmul(out[:, 0:OUT_V], chT[:, 0, cols], w_a[:, :], start=True, stop=False, skip_group_check=True)
                        if attention:
                            t.matmul(out[:, OUT_S:OUT_V], ones3[:, :], bias3[:, 1, 0:ls], start=False, stop=False,
                                     skip_group_check=True)
                        t.matmul(out[:, OUT_S:OUT_V + VD], chT[:, 1, cols], w_b[:, :], start=False, stop=False,
                                 skip_group_check=True)
                        last = t.matmul(out[:, OUT_V:OUT_V + VD], chT[0:VD, 2, cols], w_c[:, :], start=False, stop=True,
                                        skip_group_check=True)
                    last.then_inc(lin_done, 1)

                def aggregate(k, h):
                    pe.wait_ge(post_done, k + 1)
                    pe.wait_ge(acc_done, UNIT * k + 1)
                    for pair, bank in enumerate((BM, BV)):
                        for n in range(2):
                            u = 2 * pair + n
                            last = t.matmul(banks[:, bank, n * mcols:n * mcols + mcols], onehot[h][:, u * P:u * P + P],
                                            msg[h][:, u, :], start=True, stop=True)
                        last.then_inc(agg_done, 1)

                pe.wait_ge(ident_ready, 1)
                pe.wait_ge(first_ready, 1)
                pe.wait_ge(prepared, 1)
                for n in range(layers):
                    net_map(0, n)
                    if norms:
                        net_var(0, n)
                if attention:
                    turn_onehot(0, 0)
                gather_and_weights(0, 0, 0)
                with pe.Fori(0, ITERS) as i:
                    now, a_, nxt = 2 * i, 2 * i + 1, 2 * i + 2
                    net_map(i + 1, 0)
                    if attention:
                        turn_onehot(a_, 1)
                        net_var(i + 1, 0)
                    gather_and_weights(a_, 1, i)
                    turn_channels(now, 0)
                    if attention:
                        net_map(i + 1, 1)
                    linear(now)
                    if attention:
                        net_var(i + 1, 1)
                        turn_onehot(nxt, 0)
                        gather(nxt, 0)
                    turn_channels(a_, 1)
                    gather_and_weights(nxt, 0, i + 1, attention)
                    if not attention:
                        aggregate(now, 0)
                    linear(a_)
                    if not attention:
                        aggregate(a_, 1)

            @block.scalar
            def _(act):
                s = nc.scalar
                s.preload_act_table_set(TABLES)

                def square(j, n):
                    act.wait_ge(x_done, layers * j + n + 1)
                    s.activation(sq[:, :], banks[:, BX, :], ACT.Square, bias=net_cols[:, n, 0:1]).then_inc(sq_done, 1)

                def inverse_deviation(j, n):
                    act.wait_ge(v_done, layers * j + n + 1)
                    s.activation(rs[:, :], banks[:, BV, :], ACT.Ln, bias=net_cols[:, n, 3:4]).then_inc(log_done, 1)
                    act.wait_ge(log_done, layers * j + n + 1)
                    s.activation(rs[:, :], rs[:, :], ACT.Exp, scale=-0.5).then_inc(rs_done, 1)

                def sigmoid(j, n, between=lambda pair: None):
                    count = layers * j + n + 1
                    if norms:
                        act.wait_ge(z_done, count)
                    else:
                        act.wait_ge(x_done, count)
                        at_least(act, h_done, count - 1)
                    s.activation(e[:, :], z[:, :] if norms else banks[:, BX, :], ACT.Exp, scale=-1.0).then_inc(e_done, 1)
                    between(0)
                    act.wait_ge(e_done, count)
                    s.activation(e[:, :], e[:, :], ACT.Ln, bias=1.0).then_inc(u_done, 1)
                    between(1)
                    act.wait_ge(u_done, count)
                    s.activation(e[:, :], e[:, :], ACT.Exp, scale=-1.0).then_inc(r_done, 1)

                def onehot_out(k, h):
                    act.wait_ge(ohT_done, k + 1)
                    s.activation(onehotT[:, :], banks[:, BT, :], ACT.Copy).then_inc(oht_done, 1)
                    act.wait_ge(glen_done, k + 1)
                    s.activation(glog[:, :], glen[h][:, :], ACT.Ln).then_inc(glog_done, 1)
                    act.wait_ge(glog_done, k + 1)
                    s.activation(glen[h][:, :], glog[:, :], ACT.Exp, scale=-0.5).then_inc(gr_done, 1)

                def weights_out(k, pairs=(0, 1)):
                    for pair in pairs:
                        if pair == 0:
                            at_least(act, prod_done, k)
                        act.wait_ge(w_done, 2 * k + pair + 1)
                        s.activation(wS[:, 2 * pair:2 * pair + 2, :],
                                     banks[:, BW, 0:2 * WN].rearrange("p (u c) -> p u c", u=2), ACT.Copy)\
                            .then_inc(wev_done, 1)

                def channels_out(k):
                    for c, rows in enumerate((P, P, VD)):
                        act.wait_ge(bt_done, 3 * k + c + 1)
                        s.activation(chT[0:rows, c, :], banks[0:rows, BT + c % 2, :], ACT.Copy).then_inc(bev_done, 1)

                def scalars_out(k, h, i):
                    act.wait_ge(lin_done, k + 1)
                    if attention:
                        act.wait_ge(msg_stored[h], 16 * (i + 1))
                    for pair in range(2):
                        bank = banks[:, BL + pair, :].rearrange("p (u c) -> p u c", u=2)
                        us = slice(2 * pair, 2 * pair + 2)
                        if attention:
                            s.activation(ea[:, us, :], bank[:, :, OUT_S:OUT_S + S], ACT.Exp, scale=-1.0).then_inc(ea_done, 1)
                            last = s.activation(msg[h][:, us, 0:S], bank[:, :, OUT_S + S:OUT_V], ACT.Copy)
                        else:
                            last = s.activation(msg[h][:, us, 0:ls], bank[:, :, OUT_S:OUT_V], ACT.Copy)
                    last.then_inc(act_post, 1)
                    if attention:
                        act.wait_ge(ea_done, 2 * k + 2)
                        s.activation(ea[:, :, :], ea[:, :, :], ACT.Ln, bias=1.0).then_inc(u2_done, 1)
                        act.wait_ge(u2_done, k + 1)
                        s.activation(ea[:, :, :], ea[:, :, :], ACT.Exp, scale=-1.0).then_inc(r2_done, 1)

                act.wait_ge(prepared, 1)
                for n in range(layers):
                    if norms:
                        square(0, n)
                        inverse_deviation(0, n)
                    sigmoid(0, n)
                if attention:
                    onehot_out(0, 0)
                weights_out(0)
                with act.Fori(0, ITERS) as i:
                    now, a_, nxt = 2 * i, 2 * i + 1, 2 * i + 2
                    if attention:
                        square(i + 1, 0)
                        onehot_out(a_, 1)
                        inverse_deviation(i + 1, 0)
                        sigmoid(i + 1, 0, lambda pair: weights_out(a_, (pair,)))
                        channels_out(now)
                        square(i + 1, 1)
                        scalars_out(now, 0, i)
                        inverse_deviation(i + 1, 1)
                        onehot_out(nxt, 0)
                        sigmoid(i + 1, 1)
                    else:
                        sigmoid(i + 1, 0)
                        weights_out(a_)
                        channels_out(now)
                        scalars_out(now, 0, i)
                    channels_out(a_)
                    weights_out(nxt)
                    scalars_out(a_, 1, i)

            @block.vector
            def _(dve):
                v = nc.vector
                c = Chain(dve, prep_chain)
                for h in range(2):
                    r = slice(h * S, h * S + S)
                    v.memset(mean[r, r], 1.0 / S)
                    v.memset(mean[r, (1 - h) * S:(2 - h) * S], 0.0)
                for t in net:
                    c.link(v.memset(t[:, :], 0.0))
                dve.wait_ge(first_ready, 1)
                if attention:
                    for n in range(2):
                        for h in range(2):
                            r = slice(h * S, h * S + S)
                            c.link(v.tensor_reduce(rowsum[r, n, 0:1], net[n][r, r], AX.X, ALU.add))
                            c.link(v.tensor_scalar(rowsum[r, n, 1:2], rowsum[r, n, 0:1], -1.0 / S, None, ALU.mult))
                            c.link(v.tensor_scalar(net[n][r, r], net[n][r, r], rowsum[r, n, 1:2], None, ALU.add))
                        v.memset(net_cols[:, n, 3:4], EPS)
                    c.link(v.tensor_scalar(w_a[S:2 * S, 0:V], w_a[S:2 * S, 0:V], float(np.sqrt(3.0)), None, ALU.mult))
                    c.link(v.tensor_scalar(w_c[:, :], w_c[:, :], float(np.sqrt(1.5)), None, ALU.mult))
                    c.link(v.tensor_scalar(adot[:, :], adot[:, :], 0.8, None, ALU.mult))
                    c.link(v.tensor_copy(bias3[:, :, :], rows3[:, :, :]))
                    for part in range(1, 3):
                        for left in range(part, 3):
                            r = slice(left * Q, left * Q + Q)
                            c.link(v.tensor_tensor(rows3[r, :, :], rows3[r, :, :], bias3[r, :, :], ALU.subtract))
                            c.link(v.tensor_copy(bias3[r, :, :], rows3[r, :, :]))
                    for n in range(2):
                        c.link(v.tensor_reduce(rb_mean[:, n:n + 1], rb_rows[:, n, :], AX.X, ALU.add))
                        c.link(v.tensor_scalar(rb_mean[:, n:n + 1], rb_mean[:, n:n + 1], -1.0 / S, None, ALU.mult))
                        c.link(v.tensor_tensor(net_cols[:, n, 0:1], net_cols[:, n, 0:1], rb_mean[:, n:n + 1], ALU.add))
                else:
                    for h in range(2):
                        r = slice(h * S, h * S + S)
                        c.link(v.tensor_scalar(net[0][r, r], net[0][r, r], float(S) ** -0.5, None, ALU.mult))
                    c.link(v.tensor_scalar(w_last[:, :], w_last[:, :], float(S) ** -0.5, None, ALU.mult))
                    f_s, f_v = 0.25 * float(S + V) ** -0.5, 0.25 * float(4 * V) ** -0.5
                    c.link(v.tensor_scalar(w_a[0:S, :], w_a[0:S, :], f_s, None, ALU.mult))
                    c.link(v.tensor_scalar(w_a[S:P, :], w_a[S:P, :], f_v, None, ALU.mult))
                    c.link(v.tensor_scalar(w_b[0:VD, :], w_b[0:VD, :], f_v, None, ALU.mult))
                    c.link(v.tensor_scalar(w_b[VD:P, :], w_b[VD:P, :], f_s * 3.0 ** -0.5, None, ALU.mult))
                    c.link(v.tensor_scalar(w_c[:, :], w_c[:, :], f_v * 2.0 ** -0.5, None, ALU.mult))
                    v.memset(sums[:, :, :], 0.0).then_inc(acc_done, 1)
                v.memset(rowsum[:, :, :], 0.0).then_inc(prepared, 1)

                def one_hots(k, h, i):
                    dve.wait_ge(idx_landed[h], 16 * UNIT * (i + 1))
                    v.tensor_copy(dstf[:, :], idx[h][:, :, 1]).then_inc(df_done, 1)
                    dve.wait_ge(df_done, k + 1)
                    v.tensor_tensor(rel[:, :], dstf[:, :], base[:, bass.ds(UNIT * k, UNIT)], ALU.subtract).then_inc(rel_done, 1)
                    dve.wait_ge(rel_done, k + 1)
                    for u in range(UNIT):
                        last = v.tensor_scalar(onehot[h][:, u * P:u * P + P], number[:, :], rel[:, u:u + 1], None, ALU.is_equal)
                    last.then_inc(oh_done, 1)
                    if attention:
                        v.tensor_scalar(valid[:, 0, :], rel[:, :], 0.0, None, ALU.is_ge).then_inc(val_done, 1)
                        dve.wait_ge(val_done, 2 * k + 1)
                        v.scalar_tensor_tensor(valid[:, 1, :], rel[:, :], float(P - 1), valid[:, 0, :],
                                               ALU.is_le, ALU.mult).then_inc(val_done, 1)
                        dve.wait_ge(val_done, 2 * k + 2)
                        v.scalar_tensor_tensor(dkey[h][:, :], dstf[:, :], 1.0, valid[:, 1, :],
                                               ALU.add, ALU.mult).then_inc(key_done, 1)
                        dve.wait_ge(geo_landed[h], 16 * UNIT * (i + 1))
                        v.tensor_tensor(gsq[:, :, :], geo[h][:, :, :], geo[h][:, :, :], ALU.mult).then_inc(gsq_done, 1)
                        dve.wait_ge(gsq_done, 2 * k + 1)
                        v.tensor_reduce(glen[h][:, :], gsq[:, :, :], AX.X, ALU.add).then_inc(gsq_done, 1)
                        dve.wait_ge(gsq_done, 2 * k + 2)
                        v.tensor_scalar(glen[h][:, :], glen[h][:, :], 1e-12, None, ALU.add).then_inc(glen_done, 1)

                def normalise(j, n):
                    dve.wait_ge(rs_done, layers * j + n + 1)
                    v.scalar_tensor_tensor(xn[:, :], banks[:, BX, :], net_cols[:, n, 0:1], rs[:, :],
                                           ALU.add, ALU.mult).then_inc(xn_done, 1)
                    dve.wait_ge(xn_done, layers * j + n + 1)
                    v.tensor_scalar(z[:, :], xn[:, :], net_cols[:, n, 1:2], net_cols[:, n, 2:3],
                                    ALU.mult, ALU.add).then_inc(z_done, 1)

                def silu(j, n):
                    dve.wait_ge(r_done, layers * j + n + 1)
                    v.tensor_tensor(hid[n][:, :], z[:, :] if norms else banks[:, BX, :], e[:, :], ALU.mult)\
                        .then_inc(h_done, 1)

                def endpoints(k, h, i):
                    dve.wait_ge(src_landed[h], 16 * UNIT * (i + 1))
                    if attention:
                        at_least(dve, prod_done, k)
                        dve.wait_ge(gr_done, k + 1)
                        r = bc(glen[h][:, :], 2, D)
                        v.tensor_tensor(yx[h][:, :, 0:D], geo[h][:, :, :], r, ALU.mult)
                        v.tensor_tensor(yx[h][:, :, D:5], geo[h][:, :, 0:2], r[:, :, 0:2], ALU.mult).then_inc(yx_done, 1)
                        for pair in range(2):
                            dve.wait_ge(m_done, 2 * k + pair + 1)
                            us = slice(2 * pair, 2 * pair + 2)
                            v.tensor_tensor(m[:, us, :], banks[:, BM, 0:2 * FEAT].rearrange("p (u c) -> p u c", u=2),
                                            src[h][:, us, :], ALU.add).then_inc(madd_done, 1)
                    else:
                        at_least(dve, prod_done, k)
                        dve.wait_ge(geo_landed[h], 16 * UNIT * (i + 1))
                        v.tensor_copy(yx[h][:, :, 0:D], geo[h][:, :, 1:1 + D])
                        v.tensor_copy(yx[h][:, :, D:5], geo[h][:, :, 1:3]).then_inc(yx_done, 1)
                        v.tensor_tensor(m[:, :, :], src[h][:, :, :], bc(geo[h][:, :, 0], 2, FEAT), ALU.mult)\
                            .then_inc(madd_done, 1)

                def products(k, h):
                    raw = m if attention else src[h]
                    dve.wait_ge(madd_done, (2 if attention else 1) * (k + 1))
                    dve.wait_ge(yx_done, k + 1)
                    mv = raw[:, :, S:FEAT].rearrange("p u (c d) -> p u c d", d=D)
                    y = yx[h]
                    v.tensor_tensor(p0[:, :, :, :], mv, bc(y[:, :, 0:3], 2, V), ALU.mult).then_inc(p_done, 1)
                    v.tensor_tensor(p1[:, :, :, :], mv, bc(y[:, :, 1:4], 2, V), ALU.mult)
                    v.tensor_tensor(p2[:, :, :, :], mv, bc(y[:, :, 2:5], 2, V), ALU.mult).then_inc(p_done, 1)
                    dve.wait_ge(p_done, 2 * k + 2)
                    v.tensor_reduce(dot[:, :, :], p0[:, :, :, :], AX.X, ALU.add).then_inc(dot_done, 1)
                    dve.wait_ge(dot_done, k + 1)
                    for d in range(D):
                        last = v.tensor_tensor(p0[:, :, :, d], p1[:, :, :, (d + 1) % 3], p2[:, :, :, (d + 2) % 3], ALU.subtract)
                    last.then_inc(cross_done, 1)

                def weigh(k, h):
                    dve.wait_ge(wev_done, 2 * k + 2)
                    if attention:
                        v.tensor_tensor(ch[h][:, :, 0:C3].rearrange("p u (a c) -> p u a c", a=2),
                                        wS[:, :, 0:C3].rearrange("p u (a c) -> p u a c", a=2),
                                        bc(m[:, :, 0:S], 2, 2), ALU.mult)
                    else:
                        v.tensor_tensor(ch[h][:, :, 0:S], wS[:, :, 0:S], m[:, :, 0:S], ALU.mult)
                        v.tensor_tensor(ch[h][:, :, S:C3], wS[:, :, S:C3], src[h][:, :, 0:S], ALU.mult)
                    v.tensor_tensor(ch[h][:, :, C3:C4].rearrange("p u (c d) -> p u c d", d=D),
                                    m[:, :, S:FEAT].rearrange("p u (c d) -> p u c d", d=D),
                                    bc(wS[:, :, 2 * S:2 * S + V], 3, D), ALU.mult)
                    v.tensor_tensor(ch[h][:, :, C4:C5], dot[:, :, :], wS[:, :, 2 * S + V:2 * S + 2 * V], ALU.mult)
                    dve.wait_ge(cross_done, k + 1)
                    v.tensor_tensor(ch[h][:, :, C5:CHAN].rearrange("p u (c d) -> p u c d", d=D), p0[:, :, :, :],
                                    bc(wS[:, :, 2 * S + 2 * V:WN], 3, D), ALU.mult).then_inc(prod_done, 1)

                def keep_key(h, i):
                    dve.wait_ge(key_stored[h], 16 * (i + 1))
                    v.tensor_copy(key[h][:, :, HEADS], dkey[h][:, :])

                def finish(k, h):
                    dve.wait_ge(act_post, k + 1)
                    for pair in range(2):
                        bank = banks[:, BL + pair, :].rearrange("p (u c) -> p u c", u=2)
                        us = slice(2 * pair, 2 * pair + 2)
                        last = v.tensor_tensor(ty[:, us, :, :], bc(bank[:, :, OUT_A:OUT_A + V], 3, D),
                                               bc(yx[h][:, us, 0:D], 2, V), ALU.mult)
                    last.then_inc(ty_done, 1)
                    dve.wait_ge(ty_done, k + 1)
                    vec0 = S if attention else ls
                    for pair in range(2):
                        bank = banks[:, BL + pair, :].rearrange("p (u c) -> p u c", u=2)
                        us = slice(2 * pair, 2 * pair + 2)
                        last = v.tensor_tensor(msg[h][:, us, vec0:mcols], bank[:, :, OUT_V:OUT_V + VD],
                                               ty[:, us, :, :].rearrange("p u c d -> p u (c d)"), ALU.add)
                    if not attention:
                        last.then_inc(post_done, 1)
                        return
                    dve.wait_ge(r2_done, k + 1)
                    for pair in range(2):
                        bank = banks[:, BL + pair, :].rearrange("p (u c) -> p u c", u=2)
                        us = slice(2 * pair, 2 * pair + 2)
                        last = v.scalar_tensor_tensor(ra[:, us, :], ea[:, us, :], 0.25, bank[:, :, OUT_S:OUT_S + S],
                                                      ALU.add, ALU.mult)
                    last.then_inc(sl_done, 1)
                    dve.wait_ge(sl_done, k + 1)
                    v.tensor_tensor(ea[:, :, :], ra[:, :, :], bc(adot[:, :], 1, UNIT), ALU.mult).then_inc(ad_done, 1)
                    dve.wait_ge(ad_done, k + 1)
                    v.tensor_reduce(key[h][:, :, 0:HEADS], ea[:, :, :].rearrange("p u (n c) -> p u n c", n=HEADS),
                                    AX.X, ALU.add).then_inc(post_done, 1)

                def accumulate(k):
                    bs = [dve.value_load(blocks_sb[0:1, bass.ds(UNIT * k + u, 1)], min_val=0, max_val=BLOCKS)
                          for u in range(UNIT)]
                    for u in range(UNIT):
                        if u % 2 == 0:
                            dve.wait_ge(agg_done, 2 * k + u // 2 + 1)
                        at = sums[:, bass.ds(bs[u], 1), :].rearrange("p a f -> p (a f)")
                        dve.wait_ge(acc_done, UNIT * k + u + 1)
                        v.tensor_tensor(at, at, banks[:, (BM, BV)[u // 2], u % 2 * mcols:u % 2 * mcols + mcols],
                                        ALU.add).then_inc(acc_done, 1)

                one_hots(0, 0, 0)
                if attention:
                    one_hots(1, 1, 0)
                for n in range(layers):
                    if norms:
                        normalise(0, n)
                    silu(0, n)
                endpoints(0, 0, 0)
                products(0, 0)
                weigh(0, 0)
                with dve.Fori(0, ITERS) as i:
                    now, a_, nxt = 2 * i, 2 * i + 1, 2 * i + 2
                    if attention:
                        normalise(i + 1, 0)
                        endpoints(a_, 1, i)
                        products(a_, 1)
                        silu(i + 1, 0)
                        weigh(a_, 1)
                        keep_key(0, i)
                        one_hots(nxt, 0, i + 1)
                        finish(now, 0)
                        normalise(i + 1, 1)
                        silu(i + 1, 1)
                        endpoints(nxt, 0, i + 1)
                        products(nxt, 0)
                        weigh(nxt, 0)
                        keep_key(1, i)
                        one_hots(nxt + 1, 1, i + 1)
                        finish(a_, 1)
                    else:
                        one_hots(a_, 1, i)
                        endpoints(a_, 1, i)
                        products(a_, 1)
                        weigh(a_, 1)
                        silu(i + 1, 0)
                        finish(now, 0)
                        endpoints(nxt, 0, i + 1)
                        products(nxt, 0)
                        weigh(nxt, 0)
                        accumulate(now)
                        one_hots(nxt, 0, i + 1)
                        finish(a_, 1)
                        accumulate(a_)




def phase_softmax(nc, keyed):
    L = STEPS
    with ExitStack() as ctx:
        a = Arena(nc, ctx, "smax")
        banks = a.banks()
        ident = a.sb("ident", [P, P])
        kd = a.sb("kd", [P, L, KEYED])
        keyx = a.sb("keyx", [P, L + 2])
        pen = a.sb("pen", [P, L + 1])
        run = a.sb("run", [P, HEADS, L])
        best = a.sb("best", [P, L])
        ends = a.sb("ends", [P, 2, HEADS])
        enter = a.sb("enter", [P, HEADS])
        endsT = a.sb("endsT", [HEADS, 2, P])
        carry = a.sb("carry", [HEADS, P + 1])
        (cleared, ident_ready, edge_set, loaded, chain, ends_ready, ends_turned, carried, enter_turned, shifted,
         exped, stored) = (a.sem(n) for n in (
             "cleared", "ident_ready", "edge_set", "loaded", "chain", "ends_ready", "ends_turned", "carried",
             "enter_turned", "shifted", "exped", "stored"))
        rows = keyed.rearrange("(q l) f -> q l f", l=L)
        with nc.Block() as block:
            @block.gpsimd
            def _(pool):
                make_identity(nc, pool, ident, cleared, ident_ready)
                nc.gpsimd.memset(keyx[:, :], -1.0).then_inc(edge_set, 1)

            @block.sync
            def _(sp):
                sp.dma_start(kd[:, :, :], rows).then_inc(loaded, 16)
                sp.wait_ge(edge_set, 1)
                sp.dma_start(keyx[1:P, 0:1], rows[0:P - 1, L - 1, HEADS:KEYED],
                             allow_slow_non_contiguous=True).then_inc(loaded, 16)
                sp.dma_start(keyx[0:P - 1, L + 1:L + 2], rows[1:P, 0, HEADS:KEYED],
                             allow_slow_non_contiguous=True).then_inc(loaded, 16)
                sp.wait_ge(exped, 1)
                sp.dma_start(rows, kd[:, :, :]).then_inc(stored, 16)
                sp.wait_ge(stored, 16)

            @block.vector
            def _(dve):
                v = nc.vector
                c = Chain(dve, chain)
                dve.wait_ge(loaded, 48)
                c.link(v.tensor_copy(keyx[:, 1:L + 1], kd[:, :, HEADS]))
                c.link(v.tensor_tensor(pen[:, :], keyx[:, 1:L + 2], keyx[:, 0:L + 1], ALU.not_equal))
                c.link(v.tensor_scalar(pen[:, :], pen[:, :], -BIG, None, ALU.mult))
                for turn in range(2):
                    lo = turn
                    way = slice(None, None, -1) if turn else slice(None)
                    p_ = pen[:, lo:lo + L][:, way]

                    def values(h):
                        return run[:, h, :][:, way] if turn else kd[:, :, h]

                    for h in range(HEADS):
                        c.link(v.tensor_tensor_scan(best[:, way], p_, values(h), -BIG, ALU.add, ALU.max))
                        c.link(v.tensor_copy(ends[:, 0, h:h + 1], best[:, 0:1] if turn else best[:, L - 1:L]))
                    c.link(v.tensor_reduce(ends[:, 1, 0:1], pen[:, lo:lo + L], AX.X, ALU.add))
                    v.tensor_copy(ends[:, 1, 1:HEADS], ends[:, 1, 0:1].broadcast_to([P, HEADS - 1])).then_inc(ends_ready, 1)
                    dve.wait_ge(ends_turned, turn + 1)
                    c.link(v.tensor_copy(endsT[:, :, :], banks[0:HEADS, 0, 0:2 * P].rearrange("p (a q) -> p a q", a=2)))
                    c.link(v.memset(carry[:, :], -BIG))
                    out = carry[:, 0:P][:, way] if turn else carry[:, 1:P + 1]
                    v.tensor_tensor_scan(out, endsT[:, 1, way], endsT[:, 0, way], -BIG, ALU.add, ALU.max).then_inc(carried, 1)
                    dve.wait_ge(enter_turned, turn + 1)
                    c.link(v.tensor_copy(enter[:, :], banks[:, 1, 0:HEADS]))
                    for h in range(HEADS):
                        out = best[:, way] if turn else run[:, h, :]
                        c.link(v.tensor_tensor_scan(out, p_, values(h), enter[:, h:h + 1], ALU.add, ALU.max))
                        if turn:
                            last = v.tensor_tensor(kd[:, :, h], kd[:, :, h], best[:, :], ALU.subtract)
                            if h < HEADS - 1:
                                c.link(last)
                last.then_inc(shifted, 1)

            @block.tensor
            def _(pe):
                t = nc.tensor
                pe.wait_ge(ident_ready, 1)
                for turn in range(2):
                    pe.wait_ge(ends_ready, turn + 1)
                    for n in range(2):
                        last = t.transpose(banks[0:HEADS, 0, n * P:n * P + P], ends[:, n, :], ident[:, :])
                    last.then_inc(ends_turned, 1)
                    pe.wait_ge(carried, turn + 1)
                    enters = carry[:, 1:P + 1] if turn else carry[:, 0:P]
                    t.transpose(banks[:, 1, 0:HEADS], enters, ident[0:HEADS, 0:HEADS]).then_inc(enter_turned, 1)

            @block.scalar
            def _(act):
                nc.scalar.preload_act_table_set(TABLES)
                act.wait_ge(shifted, 1)
                nc.scalar.activation(kd[:, :, 0:HEADS], kd[:, :, 0:HEADS], ACT.Exp).then_inc(exped, 1)


def phase_attend(nc, messages, keyed, step_block, step_base, sums):
    BANK = 3
    with ExitStack() as ctx:
        a = Arena(nc, ctx, "attend")
        banks = a.banks()
        number = a.sb("number", [P, P])
        base = a.sb("base", [P, TABLE])
        blocks_sb = a.sb("blocks_sb", [1, TABLE], I32)
        msg = [a.sb(f"msg{h}", [P, ITER, FEAT]) for h in range(2)]
        kd = [a.sb(f"kd{h}", [P, ITER, KEYED]) for h in range(2)]
        rel = [a.sb(f"rel{h}", [P, ITER]) for h in range(2)]
        onehot = [a.sb(f"onehot{h}", [P, ITER, P]) for h in range(2)]
        wm = [a.sb(f"wm{h}", [P, ITER, MSG]) for h in range(2)]
        (tables, numbered, rel_done, oh_done, wm_done, agg_done, acc_done, sp_passed) = (a.sem(n) for n in (
            "tables", "numbered", "rel_done", "oh_done", "wm_done", "agg_done", "acc_done", "sp_passed"))
        landed = [a.sem(f"landed{h}") for h in range(2)]
        view = keyed.rearrange("(s p) f -> p s f", p=P)
        with nc.Block() as block:
            @block.sync
            def _(sp):
                sp.dma_start(blocks_sb[:, :], row_of(step_block)).then_inc(tables, 16)
                sp.dma_start(base[:, :], spread(step_base)).then_inc(tables, 16)

                def load(j, h):
                    sp.dma_start(msg[h][:, :, :], messages[:, bass.ds(ITER * j, ITER), :]).then_inc(landed[h], 16)
                    sp.dma_start(kd[h][:, :, :], view[:, bass.ds(ITER * j, ITER), :]).then_inc(landed[h], 16)

                load(0, 0)
                load(1, 1)
                with sp.Fori(0, ITERS // 2 - 1) as i:
                    for h in range(2):
                        j = 2 * i + 2 + h
                        hold(sp, sp_passed, (wm_done, j - 1), (rel_done, j - 1))
                        load(j, h)

            @block.gpsimd
            def _(pool):
                g = nc.gpsimd
                g.iota(number[:, :], pattern=[[1, P]], base=0, channel_multiplier=0,
                       allow_small_or_imprecise_dtypes=True).then_inc(numbered, 1)

                def weigh(j, h, i):
                    pool.wait_ge(landed[h], 32 * (i + 1))
                    if not isinstance(j, int):
                        pool.wait_ge(agg_done, j - 1)
                    p_ = kd[h][:, :, 0:HEADS]
                    for lo, hi in ((0, S), (S, FEAT)):
                        n = (hi - lo) // HEADS
                        g.tensor_tensor(wm[h][:, :, lo:hi].rearrange("p u (n c) -> p u n c", n=HEADS),
                                        msg[h][:, :, lo:hi].rearrange("p u (n c) -> p u n c", n=HEADS),
                                        bc(p_, 3, n), ALU.mult)
                    g.tensor_copy(wm[h][:, :, FEAT:MSG], p_).then_inc(wm_done, 1)

                weigh(0, 0, 0)
                weigh(1, 1, 0)
                with pool.Fori(1, ITERS // 2) as i:
                    for h in range(2):
                        weigh(2 * i + h, h, i)

            @block.tensor
            def _(pe):
                t = nc.tensor

                def aggregate(j, h):
                    pe.wait_ge(oh_done, j + 1)
                    pe.wait_ge(wm_done, j + 1)
                    if not isinstance(j, int):
                        pe.wait_ge(acc_done, ITER * (j - 1))
                    for u in range(ITER):
                        last = t.matmul(banks[:, 3 * h + u // BANK, u % BANK * MSG:u % BANK * MSG + MSG],
                                        onehot[h][:, u, :], wm[h][:, u, :], start=True, stop=True)
                    last.then_inc(agg_done, 1)

                aggregate(0, 0)
                aggregate(1, 1)
                with pe.Fori(1, ITERS // 2) as i:
                    for h in range(2):
                        aggregate(2 * i + h, h)

            @block.vector
            def _(dve):
                v = nc.vector

                def one_hots(j, h, i):
                    dve.wait_ge(landed[h], 32 * (i + 1))
                    if not isinstance(j, int):
                        dve.wait_ge(agg_done, j - 1)
                    v.scalar_tensor_tensor(rel[h][:, :], kd[h][:, :, HEADS], -1.0, base[:, bass.ds(ITER * j, ITER)],
                                           ALU.add, ALU.subtract).then_inc(rel_done, 1)
                    dve.wait_ge(rel_done, j + 1)
                    for u in range(ITER):
                        last = v.tensor_scalar(onehot[h][:, u, :], number[:, :], rel[h][:, u:u + 1], None, ALU.is_equal)
                    last.then_inc(oh_done, 1)

                def accumulate(j, h):
                    dve.wait_ge(agg_done, j + 1)
                    for u in range(ITER):
                        b = dve.value_load(blocks_sb[0:1, bass.ds(ITER * j + u, 1)], min_val=0, max_val=BLOCKS)
                        at = sums[:, bass.ds(b, 1), :].rearrange("p a f -> p (a f)")
                        dve.wait_ge(acc_done, ITER * j + u + 1)
                        v.tensor_tensor(at, at, banks[:, 3 * h + u // BANK, u % BANK * MSG:u % BANK * MSG + MSG],
                                        ALU.add).then_inc(acc_done, 1)

                dve.wait_ge(tables, 32)
                dve.wait_ge(numbered, 1)
                v.memset(sums[:, :, :], 0.0).then_inc(acc_done, 1)
                one_hots(0, 0, 0)
                with dve.Fori(0, ITERS // 2 - 1) as i:
                    one_hots(2 * i + 1, 1, i)
                    accumulate(2 * i, 0)
                    one_hots(2 * i + 2, 0, i + 1)
                    accumulate(2 * i + 1, 1)
                one_hots(ITERS - 1, 1, ITERS // 2 - 1)
                accumulate(ITERS - 2, 0)
                accumulate(ITERS - 1, 1)


def phase_nodes_mid(nc, x, attr, w, w1, sums, x_mid, src_table):
    F1 = 2 * P + S
    F1S, F1V = P + S, S * D
    with ExitStack() as ctx:
        a = Arena(nc, ctx, "mid")
        banks = a.banks()
        ident = a.sb("ident", [P, P])
        proj_s, proj_v, proj_b = a.sb("proj_s", [S, S]), a.sb("proj_v", [VD, VD]), a.sb("proj_b", [P, S])
        f1_s, f1_v, f1_b = a.sb("f1_s", [S, F1S]), a.sb("f1_v", [VD, F1V]), a.sb("f1_b", [P, F1S])
        f2_s, f2_v, f2_b = a.sb("f2_s", [P, S]), a.sb("f2_v", [VD, 2, VD]), a.sb("f2_b", [P, S])
        l1_s, l1_v = a.sb("l1_s", [S, S]), a.sb("l1_v", [VD, VD])
        g_s, b_s, g_v = a.sb("g_s", [S, 1]), a.sb("b_s", [S, 1]), a.sb("g_v", [VD, 1])
        attr_sb = a.sb("attr_sb", [P, BLOCKS])
        at = a.sb("at", [P, NB])
        xb, cs, xn, x1, out = (a.sb(n, [P, NB, FEAT]) for n in ("xb", "cs", "xn", "x1", "out"))
        ff, eb = a.sb("ff", [P, NB, F1S + F1V]), a.sb("eb", [P, NB, F1S])
        mu, stat, log = a.sb("mu", [P, NB]), a.sb("stat", [P, 2, NB]), a.sb("log", [P, 2, NB])
        den = a.sb("den", [P, NB, HEADS])
        sT, vT, v2T = a.sb("sT", [P, NB * P]), a.sb("vT", [VD, NB * P]), a.sb("v2T", [VD, NB * P])
        names = ("cleared ident_ready zeroed weights x_ready chain achain ns_done turned1 out1 projected summed rooted "
                 "normed turned2 out2 mapped ffs_done exped gated turned3 out3 mapped2 summed2 rooted2 xl_done turned4 "
                 "out4 mapped3 h_done stored sp_passed").split()
        sem = {n: a.sem(n) for n in names}
        xr, xo, tr = (q.rearrange("(i j p) f -> i p j f", j=NB, p=P) for q in (x, x_mid, src_table))
        q = lambda n: sem[n]
        wait = lambda e, n, i: e.wait_ge(sem[n], i + 1)

        def bank3(first, b, n=FEAT):
            return banks[:, (first + b // 3) % 8, b % 3 * n:b % 3 * n + n]

        def groups(first, per=3):
            for g in range(0, NB, per):
                yield (first + g // per) % 8, g, min(per, NB - g)

        with nc.Block() as block:
            @block.gpsimd
            def _(pool):
                make_identity(nc, pool, ident, q("cleared"), q("ident_ready"))
                for t in (proj_v, f1_v, f2_v, l1_v):
                    last = nc.gpsimd.memset(t[:], 0.0)
                last.then_inc(q("zeroed"), 1)

            @block.sync
            def _(sp):
                done = q("weights")
                n = 0
                for dst, src in ((proj_s[:, :], w["proj_ws"]), (proj_b[:, :], spread(w["proj_bs"])),
                                 (f1_s[:, :], w["f1_ws"]), (f1_b[:, :], spread(w["f1_bs"])),
                                 (f2_s[:, :], w["f2_ws"]), (f2_b[:, :], spread(w["f2_bs"])),
                                 (l1_s[:, :], w1["lin1_ws"]), (attr_sb[:, :], attr),
                                 (g_s[:, :], col_of(w["ln2_w0"])), (b_s[:, :], col_of(w["ln2_b0"]))):
                    sp.dma_start(dst, src).then_inc(done, 16)
                    n += 16
                for d in range(D):
                    sp.dma_start(g_v[d:VD:D, :], col_of(w["ln2_w1"])).then_inc(done, 16)
                    n += 16
                sp.wait_ge(q("zeroed"), 1)
                n += load_kron(sp, done, proj_v, 0, 0, w["proj_wv"])
                n += load_kron(sp, done, f1_v, 0, 0, w["f1_wv"])
                for half in range(2):
                    n += load_kron(sp, done, f2_v[:, half, :], 0, 0, w["f2_wv"][half * V:half * V + V, :])
                n += load_kron(sp, done, l1_v, 0, 0, w1["lin1_wv"])
                sp.wait_ge(done, n)
                assert n == 16 * 28
                with sp.Fori(0, NODE_ITERS) as i:
                    sp.dma_start(xb[:, :, :], xr[i]).then_inc(q("x_ready"), 16)
                    hold(sp, q("sp_passed"), (q("xl_done"), i + 1))
                    sp.dma_start(xo[i], out[:, :, :]).then_inc(q("stored"), 16)
                    hold(sp, q("sp_passed"), (q("h_done"), i + 1))
                    sp.dma_start(tr[i], x1[:, :, :]).then_inc(q("stored"), 16)
                    hold(sp, q("sp_passed"), (q("stored"), 32 * (i + 1)))

            @block.vector
            def _(dve):
                v = nc.vector
                dve.wait_ge(q("weights"), 16 * 28)
                v.tensor_scalar(l1_s[:, :], l1_s[:, :], float(S) ** -0.5, None, ALU.mult)
                v.tensor_scalar(l1_v[:, :], l1_v[:, :], float(V) ** -0.5, None, ALU.mult)
                with dve.Fori(0, NODE_ITERS) as i:
                    c = Chain(dve, q("chain"), i, 22)
                    dve.wait_ge(q("x_ready"), 16 * (i + 1))
                    su = sums[:, bass.ds(i * NB, NB), :]
                    c.link(v.tensor_scalar(den[:, :, :], su[:, :, FEAT:MSG], 1e-12, None, ALU.add))
                    c.link(v.reciprocal(den[:, :, :], den[:, :, :]))
                    v.tensor_copy(at[:, :], attr_sb[:, bass.ds(i * NB, NB)])
                    for lo, hi in ((0, S), (S, FEAT)):
                        last = v.tensor_tensor(xn[:, :, lo:hi].rearrange("p b (n c) -> p b n c", n=HEADS),
                                               su[:, :, lo:hi].rearrange("p b (n c) -> p b n c", n=HEADS),
                                               bc(den[:, :, :], 3, (hi - lo) // HEADS), ALU.mult)
                    last.then_inc(q("ns_done"), 1)
                    wait(dve, "projected", i)
                    for bank, b, n in groups(4):
                        last = v.tensor_tensor(x1[:, b:b + n, :], banks[:, bank, 0:n * FEAT].rearrange("p (b f) -> p b f", b=n),
                                               xb[:, b:b + n, :], ALU.add)
                    c.link(last)
                    c.link(v.tensor_tensor(x1[:, :, 0:S], x1[:, :, 0:S], bc(proj_b[:, :], 1, NB), ALU.add))
                    eq_norm_sums(v, c, x1, mu, cs, out, stat).then_inc(q("summed"), 1)
                    wait(dve, "rooted", i)
                    eq_norm_apply(v, c, x1, cs, stat, xn).then_inc(q("normed"), 1)
                    wait(dve, "mapped", i)
                    for b in range(NB):
                        p = banks[:, (4 + b) % 8, :]
                        v.tensor_tensor(ff[:, b, 0:F1S], p[:, 0:F1S], f1_b[:, :], ALU.add)
                        last = v.tensor_scalar(ff[:, b, F1S:], p[:, F1S:F1S + F1V], at[:, b:b + 1], None, ALU.mult)
                    c.link(last)
                    v.tensor_tensor(ff[:, :, 0:F1S], ff[:, :, 0:F1S], bc(at[:, :], 2, F1S), ALU.mult).then_inc(q("ffs_done"), 1)
                    wait(dve, "exped", i)
                    c.link(v.tensor_scalar(eb[:, :, :], eb[:, :, :], 1.0, None, ALU.add))
                    c.link(v.reciprocal(eb[:, :, :], eb[:, :, :]))
                    v.tensor_tensor(ff[:, :, 0:P], ff[:, :, 0:P], eb[:, :, 0:P], ALU.mult)
                    for b in range(NB):
                        fv = ff[:, b, F1S:].rearrange("p (c d) -> p c d", d=D)
                        last = v.tensor_tensor(fv, fv, bc(eb[:, b, P:F1S], 2, D), ALU.mult)
                    last.then_inc(q("gated"), 1)
                    wait(dve, "mapped2", i)
                    for bank, b, n in groups(6):
                        last = v.tensor_tensor(cs[:, b:b + n, :], banks[:, bank, 0:n * FEAT].rearrange("p (b f) -> p b f", b=n),
                                               bc(at[:, b:b + n], 2, FEAT), ALU.mult)
                    c.link(last)
                    c.link(v.tensor_tensor(out[:, :, 0:S], bc(f2_b[:, :], 1, NB), bc(at[:, :], 2, S), ALU.mult))
                    c.link(v.tensor_tensor(cs[:, :, 0:S], cs[:, :, 0:S], out[:, :, 0:S], ALU.add))
                    c.link(v.tensor_tensor(cs[:, :, :], cs[:, :, :], x1[:, :, :], ALU.add))
                    c.link(v.tensor_tensor(x1[:, :, :], cs[:, :, :], xb[:, :, :], ALU.add))
                    full_norm_sums(v, c, x1, mu, cs, out, stat).then_inc(q("summed2"), 1)
                    wait(dve, "rooted2", i)
                    v.tensor_tensor(out[:, :, :], cs[:, :, :], bc(stat[:, 0, :], 2, FEAT), ALU.mult).then_inc(q("xl_done"), 1)
                    wait(dve, "mapped3", i)
                    for bank, b, n in groups(4):
                        last = v.tensor_tensor(x1[:, b:b + n, :], banks[:, bank, 0:n * FEAT].rearrange("p (b f) -> p b f", b=n),
                                               bc(at[:, b:b + n], 2, FEAT), ALU.mult)
                    last.then_inc(q("h_done"), 1)
                    c.close()

            @block.scalar
            def _(act):
                s = nc.scalar
                s.preload_act_table_set(TABLES)

                def copy_out(turned_sem, out_sem, i):
                    wait(act, turned_sem, i)
                    for p, cols in turned(banks, S, 0):
                        s.activation(sT[0:S, cols], p, ACT.Copy)
                    for p, cols in turned(banks, VD, 2):
                        last = s.activation(vT[:, cols], p, ACT.Copy)
                    last.then_inc(q(out_sem), 1)

                act.wait_ge(q("weights"), 16 * 28)
                with act.Fori(0, NODE_ITERS) as i:
                    c = Chain(act, q("achain"), i, 2)
                    copy_out("turned1", "out1", i)
                    wait(act, "summed", i)
                    inverse_root(s, c, stat[:, :, :], log[:, :, :]).then_inc(q("rooted"), 1)
                    wait(act, "turned2", i)
                    for p, cols in turned(banks, S, 0):
                        s.activation(sT[0:S, cols], p, ACT.Identity, bias=b_s[:, :], scale=g_s[:, :])
                    for p, cols in turned(banks, VD, 2):
                        last = s.activation(vT[:, cols], p, ACT.Identity, scale=g_v[:, :])
                    last.then_inc(q("out2"), 1)
                    wait(act, "ffs_done", i)
                    s.activation(eb[:, :, :], ff[:, :, 0:F1S], ACT.Exp, scale=-1.0).then_inc(q("exped"), 1)
                    wait(act, "turned3", i)
                    for first, dst, rows in ((0, sT, P), (2, vT, VD), (4, v2T, VD)):
                        for p, cols in turned(banks, rows, first):
                            last = s.activation(dst[0:rows, cols], p, ACT.Copy)
                    last.then_inc(q("out3"), 1)
                    wait(act, "summed2", i)
                    inverse_root(s, c, stat[:, 0, :], log[:, 0, :]).then_inc(q("rooted2"), 1)
                    copy_out("turned4", "out4", i)
                    c.close()

            @block.tensor
            def _(pe):
                t = nc.tensor
                pe.wait_ge(q("ident_ready"), 1)
                pe.wait_ge(q("weights"), 16 * 28)

                def two_maps(first, ws, wv, out_sem, done_sem, i):
                    wait(pe, out_sem, i)
                    for b in range(NB):
                        p = bank3(first, b)
                        cols = slice(b * P, b * P + P)
                        t.matmul(p[:, 0:S], sT[0:S, cols], ws[:, :], start=True, stop=True)
                        last = t.matmul(p[:, S:FEAT], vT[:, cols], wv[:, :], start=True, stop=True)
                    last.then_inc(q(done_sem), 1)

                with pe.Fori(0, NODE_ITERS) as i:
                    wait(pe, "ns_done", i)
                    turn_features(t, banks, xn, ident).then_inc(q("turned1"), 1)
                    two_maps(4, proj_s, proj_v, "out1", "projected", i)
                    wait(pe, "normed", i)
                    turn_features(t, banks, xn, ident).then_inc(q("turned2"), 1)
                    wait(pe, "out2", i)
                    for b in range(NB):
                        p = banks[:, (4 + b) % 8, :]
                        cols = slice(b * P, b * P + P)
                        t.matmul(p[:, 0:F1S], sT[0:S, cols], f1_s[:, :], start=True, stop=True)
                        last = t.matmul(p[:, F1S:F1S + F1V], vT[:, cols], f1_v[:, :], start=True, stop=True)
                    last.then_inc(q("mapped"), 1)
                    wait(pe, "gated", i)
                    for first, lo, hi in ((0, 0, P), (2, F1S, F1S + VD), (4, F1S + VD, F1S + 2 * VD)):
                        for b in range(NB):
                            last = t.transpose(banks[0:hi - lo, first + b // 4, b % 4 * P:b % 4 * P + P], ff[:, b, lo:hi], ident[:, :])
                    last.then_inc(q("turned3"), 1)
                    wait(pe, "out3", i)
                    for b in range(NB):
                        p = bank3(6, b)
                        cols = slice(b * P, b * P + P)
                        t.matmul(p[:, 0:S], sT[:, cols], f2_s[:, :], start=True, stop=True)
                        t.matmul(p[:, S:FEAT], vT[:, cols], f2_v[:, 0, :], start=True, stop=False)
                        last = t.matmul(p[:, S:FEAT], v2T[:, cols], f2_v[:, 1, :], start=False, stop=True)
                    last.then_inc(q("mapped2"), 1)
                    wait(pe, "xl_done", i)
                    turn_features(t, banks, out, ident).then_inc(q("turned4"), 1)
                    two_maps(4, l1_s, l1_v, "out4", "mapped3", i)


def phase_nodes_out(nc, x_mid, attr, w1, sums, y):
    M = S + V + VD
    with ExitStack() as ctx:
        a = Arena(nc, ctx, "out")
        banks = a.banks()
        ident = a.sb("ident", [P, P])
        sc_s, sc_v = a.sb("sc_s", [S, S + V]), a.sb("sc_v", [VD, VD])
        attr_sb, at = a.sb("attr_sb", [P, BLOCKS]), a.sb("at", [P, NB])
        xb, cs, sq, x1 = (a.sb(n, [P, NB, FEAT]) for n in ("xb", "cs", "sq", "x1"))
        pre, eb = a.sb("pre", [P, NB, M]), a.sb("eb", [P, NB, S + V])
        mu, stat, log = a.sb("mu", [P, NB]), a.sb("stat", [P, 2, NB]), a.sb("log", [P, 2, NB])
        sT, vT = a.sb("sT", [S, NB * P]), a.sb("vT", [VD, NB * P])
        names = ("cleared ident_ready zeroed weights scaled x_ready chain achain turned1 out1 mapped pre_done exped "
                 "summed rooted y_done stored sp_passed").split()
        sem = {n: a.sem(n) for n in names}
        q = lambda n: sem[n]
        wait = lambda e, n, i: e.wait_ge(sem[n], i + 1)
        xr, yr = (r.rearrange("(i j p) f -> i p j f", j=NB, p=P) for r in (x_mid, y))
        W = 16 * 6
        with nc.Block() as block:
            @block.gpsimd
            def _(pool):
                make_identity(nc, pool, ident, q("cleared"), q("ident_ready"))
                nc.gpsimd.memset(sc_v[:, :], 0.0).then_inc(q("zeroed"), 1)

            @block.sync
            def _(sp):
                sp.dma_start(sc_s[:, :], w1["sc_ws"]).then_inc(q("weights"), 16)
                sp.dma_start(attr_sb[:, :], attr).then_inc(q("weights"), 16)
                sp.wait_ge(q("zeroed"), 1)
                load_kron(sp, q("weights"), sc_v, 0, 0, w1["sc_wv"])
                sp.wait_ge(q("weights"), 80)
                with sp.Fori(0, NODE_ITERS) as i:
                    sp.dma_start(xb[:, :, :], xr[i]).then_inc(q("x_ready"), 16)
                    hold(sp, q("sp_passed"), (q("y_done"), i + 1))
                    sp.dma_start(yr[i], x1[:, :, :]).then_inc(q("stored"), 16)
                    hold(sp, q("sp_passed"), (q("stored"), 16 * (i + 1)))

            @block.vector
            def _(dve):
                v = nc.vector
                dve.wait_ge(q("weights"), 80)
                v.tensor_scalar(sc_s[:, :], sc_s[:, :], float(S) ** -0.5, None, ALU.mult)
                v.tensor_scalar(sc_v[:, :], sc_v[:, :], float(V) ** -0.5, None, ALU.mult).then_inc(q("scaled"), 1)
                with dve.Fori(0, NODE_ITERS) as i:
                    c = Chain(dve, q("chain"), i, 10)
                    su = sums[:, bass.ds(i * NB, NB), :]
                    v.tensor_copy(at[:, :], attr_sb[:, bass.ds(i * NB, NB)])
                    wait(dve, "mapped", i)
                    for g in range(0, NB, 2):
                        n = min(2, NB - g)
                        last = v.tensor_tensor(pre[:, g:g + n, :], banks[:, 4 + g // 2, 0:n * M].rearrange("p (b f) -> p b f", b=n),
                                               su[:, g:g + n, :], ALU.add)
                    c.link(last)
                    v.tensor_tensor(pre[:, :, :], pre[:, :, :], bc(at[:, :], 2, M), ALU.mult).then_inc(q("pre_done"), 1)
                    wait(dve, "exped", i)
                    c.link(v.tensor_scalar(eb[:, :, :], eb[:, :, :], 1.0, None, ALU.add))
                    c.link(v.reciprocal(eb[:, :, :], eb[:, :, :]))
                    v.tensor_tensor(sq[:, :, 0:S], pre[:, :, 0:S], eb[:, :, 0:S], ALU.mult)
                    c.link(v.tensor_tensor(sq[:, :, S:FEAT].rearrange("p b (c d) -> p b c d", d=D),
                                           pre[:, :, S + V:M].rearrange("p b (c d) -> p b c d", d=D),
                                           bc(eb[:, :, S:S + V], 3, D), ALU.mult))
                    dve.wait_ge(q("x_ready"), 16 * (i + 1))
                    c.link(v.tensor_tensor(x1[:, :, :], sq[:, :, :], xb[:, :, :], ALU.add))
                    full_norm_sums(v, c, x1, mu, cs, sq, stat).then_inc(q("summed"), 1)
                    wait(dve, "rooted", i)
                    v.tensor_tensor(x1[:, :, :], cs[:, :, :], bc(stat[:, 0, :], 2, FEAT), ALU.mult).then_inc(q("y_done"), 1)
                    c.close()

            @block.scalar
            def _(act):
                s = nc.scalar
                s.preload_act_table_set(TABLES)
                with act.Fori(0, NODE_ITERS) as i:
                    c = Chain(act, q("achain"), i, 1)
                    wait(act, "turned1", i)
                    for p, cols in turned(banks, S, 0):
                        s.activation(sT[:, cols], p, ACT.Copy)
                    for p, cols in turned(banks, VD, 2):
                        last = s.activation(vT[:, cols], p, ACT.Copy)
                    last.then_inc(q("out1"), 1)
                    wait(act, "pre_done", i)
                    s.activation(eb[:, :, :], pre[:, :, 0:S + V], ACT.Exp, scale=-1.0).then_inc(q("exped"), 1)
                    wait(act, "summed", i)
                    inverse_root(s, c, stat[:, 0, :], log[:, 0, :]).then_inc(q("rooted"), 1)
                    c.close()

            @block.tensor
            def _(pe):
                t = nc.tensor
                pe.wait_ge(q("ident_ready"), 1)
                pe.wait_ge(q("scaled"), 1)
                with pe.Fori(0, NODE_ITERS) as i:
                    pe.wait_ge(q("x_ready"), 16 * (i + 1))
                    turn_features(t, banks, xb, ident).then_inc(q("turned1"), 1)
                    wait(pe, "out1", i)
                    for b in range(NB):
                        p = banks[:, 4 + b // 2, b % 2 * M:b % 2 * M + M]
                        cols = slice(b * P, b * P + P)
                        t.matmul(p[:, 0:S + V], sT[:, cols], sc_s[:, :], start=True, stop=True)
                        last = t.matmul(p[:, S + V:M], vT[:, cols], sc_v[:, :], start=True, stop=True)
                    last.then_inc(q("mapped"), 1)


L0 = ["ln1_w0", "ln1_b0", "ln1_w1", "ln2_w0", "ln2_b0", "ln2_w1", "msrc_ws", "msrc_wv", "mdst_ws", "mdst_bs",
      "mdst_wv", "rw1", "rb1", "rg1", "rbe1", "rw2", "rb2", "rg2", "rbe2", "rw3", "roff", "lin_ws", "lin_bs",
      "lin_wv", "alpha_dot", "proj_ws", "proj_bs", "proj_wv", "f1_ws", "f1_bs", "f1_wv", "f2_ws", "f2_bs", "f2_wv"]
L1 = ["lin1_ws", "lin1_wv", "fc_w1", "fc_w2", "sc_ws", "sc_wv", "lin2_ws", "lin2_wv"]


def build(nc, t, y):
    w = {n: t["L0_gnn_" + n] for n in L0}
    w1 = {n: t["L1_gnn_" + n] for n in L1}

    def scratch(name, shape, dt=F32):
        return nc.dram_tensor(name, shape, dt, kind="Internal").ap()

    step_tile, step_block = scratch("step_tile", (TABLE,), I32), scratch("step_block", (TABLE,), I32)
    step_base = scratch("step_base", (TABLE,))
    src_table, conv_table, x_mid = (scratch(n, (BLOCKS * P, FEAT)) for n in ("src_table", "conv_table", "x_mid"))
    messages = scratch("messages", (P, STEPS, FEAT))
    keyed = scratch("keyed", (STEPS * P, KEYED))
    phase_steps(nc, t["dst_first"], t["dst_last"], step_tile, step_block, step_base)
    with nc.sbuf_tensor("dst_feat", [P, BLOCKS + 1, FEAT], F32) as dst_feat:
        phase_nodes_in(nc, t["x"], w, src_table, dst_feat)
        phase_edges(nc, True, src_table, t["esT"], t["src_dst"], t["edge_vec"], step_tile, step_block, step_base,
                    dict(net=[w["rw1"], w["rw2"]], w_last=w["rw3"], rb=[w["rb1"], w["rb2"]], rg=[w["rg1"], w["rg2"]],
                         rbe=[w["rbe1"], w["rbe2"]], roff=w["roff"], lin_ws=w["lin_ws"], lin_bs=w["lin_bs"],
                         lin_wv=w["lin_wv"], adot=w["alpha_dot"]),
                    dst_feat=dst_feat, messages=messages, keyed=keyed.rearrange("(s p) f -> p s f", p=P))
    phase_softmax(nc, keyed)
    with nc.sbuf_tensor("att_sums", [P, BLOCKS + 1, MSG], F32) as sums:
        phase_attend(nc, messages, keyed, step_block, step_base, sums)
        phase_nodes_mid(nc, t["x"], t["attr"], w, w1, sums, x_mid, conv_table)
    with nc.sbuf_tensor("conv_sums", [P, BLOCKS + 1, S + V + VD], F32) as sums:
        phase_edges(nc, False, conv_table, t["esT"], t["src_dst"], t["edge_attr"], step_tile, step_block, step_base,
                    dict(net=[w1["fc_w1"]], w_last=w1["fc_w2"], lin_ws=w1["lin2_ws"], lin_wv=w1["lin2_wv"]), sums=sums)
        phase_nodes_out(nc, x_mid, t["attr"], w1, sums, y)


def kernel(**inputs):
    import concourse.bacc as bacc
    from concourse.bass_utils import run_bass_kernel_spmd

    def padded(a, rows, fill=0):
        a = np.ascontiguousarray(a)
        out = np.full((rows,) + a.shape[1:], fill, a.dtype)
        out[:a.shape[0]] = a
        return out

    E, N = TILES * P, BLOCKS * P
    src, dst = padded(inputs["src"], E), padded(inputs["dst"], E, NODES)
    arrays = {
        "x": padded(inputs["x"], N),
        "attr": np.ascontiguousarray(padded(inputs["node_vec1"], N).reshape(BLOCKS, P).T),
        "src_dst": np.ascontiguousarray(np.stack([src, dst], axis=1)).reshape(TILES, P, 2),
        "dst_first": np.ascontiguousarray(dst[0::P]),
        "dst_last": np.ascontiguousarray(dst[P - 1::P]),
        "esT": np.ascontiguousarray(padded(inputs["edge_attr_64"], E).reshape(TILES, P, S).transpose(0, 2, 1)),
        "edge_vec": padded(inputs["edge_attr_3"], E).reshape(TILES, P, D),
        "edge_attr": padded(inputs["edge_attr_4"], E).reshape(TILES, P, D + 1),
    }
    for name in ["L0_gnn_" + n for n in L0] + ["L1_gnn_" + n for n in L1]:
        arrays[name] = np.ascontiguousarray(inputs[name])
    nc = bacc.Bacc("TRN2", target_bir_lowering=False, num_devices=1)
    tensors = {name: nc.dram_tensor("in_" + name, a.shape, mybir.dt.from_np(a.dtype), kind="ExternalInput").ap()
               for name, a in arrays.items()}
    y = nc.dram_tensor("y", (N, FEAT), F32, kind="ExternalOutput").ap()
    build(nc, tensors, y)
    r = run_bass_kernel_spmd(nc, [{"in_" + name: a for name, a in arrays.items()}], core_ids=[0])
    return r.results[0]["y"][:NODES]
```
